# Optimizing a Trainium2 kernel written in Bass

```python
import numpy as np
import jax
import jax.numpy as jnp

def _softmax(x, axis=-1):
    return jax.nn.softmax(x, axis=axis)

def _gelu(x):
    return jax.nn.gelu(x, approximate=True)

def _silu(x):
    return jax.nn.silu(x)

def _sigmoid(x):
    return jax.nn.sigmoid(x)

def _layernorm(x, axis=-1, eps=1e-05):
    m = jnp.mean(x, axis=axis, keepdims=True)
    v = jnp.var(x, axis=axis, keepdims=True)
    return (x - m) / jnp.sqrt(v + eps)

def _scatter_add(tgt, idx, src, axis=0):
    return tgt.at[idx].add(src)

def _segment_sum(src, seg, n):
    return jax.ops.segment_sum(src, seg, n)
kernel_name = 'mk_gnn_preln_d2_gnn_r32_5c7497'

def setup_inputs(seed: int=0):
    np.random.seed(seed)
    _w = jnp.asarray

    def _rec_inputs():
        import jax
        import jax.numpy as jnp
        _gk = jax.random.key(seed)
        x = -0.000202 + 1 * jax.random.normal(jax.random.fold_in(_gk, 1), (3125, 128), jnp.float32)
        _s = jax.random.randint(jax.random.fold_in(_gk, 2), (25000,), 0, 3125, jnp.int32)
        _d = jax.random.randint(jax.random.fold_in(_gk, 3), (25000,), 0, 3125, jnp.int32)
        _loop = jnp.arange(3125, dtype=jnp.int32)
        src = jnp.concatenate([_s, _d, _loop])
        dst = jnp.concatenate([_d, _s, _loop])
        _o = jnp.argsort(dst, stable=True)
        src = src[_o]
        dst = dst[_o]
        edge_attr_32 = 0.000196303 + 1.00016 * jax.random.normal(jax.random.fold_in(_gk, 11), (53125, 32), jnp.float32)
        return (x, src, dst, edge_attr_32)
    x, src, dst, edge_attr_32 = _rec_inputs()

    def _L0_gnn_setup():
        import jax, jax.numpy as jnp
        import numpy as np
        N_NODES = 50000
        N_EDGES = 25000
        D_IN = 128
        D_HID = 128
        D_OUT = 128

        def gcn_layer(x, W, b, src, dst, num_nodes):
            h = x @ W
            deg = jnp.zeros((num_nodes,), dtype=h.dtype).at[dst].add(1.0) + 1.0
            dinv = jax.lax.rsqrt(deg)
            coef = dinv[src] * dinv[dst]
            msg = h[src] * coef[:, None]
            agg = jnp.zeros_like(h).at[dst].add(msg)
            agg = agg + h * (dinv * dinv)[:, None]
            return agg + b
        key = jax.random.key(seed)
        ks = jax.random.split(key, 8)
        x = jax.random.normal(ks[0], (N_NODES, D_IN), dtype=jnp.float32)
        edge_index = jax.random.randint(ks[1], (2, N_EDGES), 0, N_NODES, dtype=jnp.int64)
        s = 0.05
        W1 = jax.random.normal(ks[2], (D_IN, D_HID), dtype=jnp.float32) * s
        b1 = jnp.zeros((D_HID,), dtype=jnp.float32)
        W2 = jax.random.normal(ks[3], (D_HID, D_HID), dtype=jnp.float32) * s
        b2 = jnp.zeros((D_HID,), dtype=jnp.float32)
        W3 = jax.random.normal(ks[4], (D_HID, D_OUT), dtype=jnp.float32) * s
        b3 = jnp.zeros((D_OUT,), dtype=jnp.float32)
        return {'x': x, 'edge_index': edge_index, 'W1': W1, 'b1': b1, 'W2': W2, 'b2': b2, 'W3': W3, 'b3': b3}
    _L0_gnn_all = _L0_gnn_setup()
    _L0_gnn_in = {k: v for k, v in _L0_gnn_all.items() if k in ('W1', 'b1', 'W2', 'b2', 'W3', 'b3')}
    del _L0_gnn_all

    def _L1_gnn_setup():
        import jax, jax.numpy as jnp
        import numpy as np
        N, H, E, EDGE_DIM, STEPS = (50000, 128, 25000, 32, 3)
        LN_EPS = 1e-05

        def _glorot(key, shape):
            fan_in, fan_out = (shape[0], shape[1])
            lim = np.sqrt(6.0 / (fan_in + fan_out)).astype(np.float32)
            return jax.random.uniform(key, shape, jnp.float32, -lim, lim)

        def _mlp(x, w1, b1, w2, b2, w3, b3):
            x = jax.nn.relu(x @ w1 + b1)
            x = jax.nn.relu(x @ w2 + b2)
            return x @ w3 + b3

        def _layernorm(x, g, b):
            mu = jnp.mean(x, axis=-1, keepdims=True)
            var = jnp.mean(jnp.square(x - mu), axis=-1, keepdims=True)
            return (x - mu) * jax.lax.rsqrt(var + LN_EPS) * g + b
        key = jax.random.key(seed)
        ks = jax.random.split(key, 12)
        h = jax.random.normal(ks[0], (N, H), jnp.float32)
        edge_index = jax.random.randint(ks[1], (2, E), 0, N, jnp.int64)
        edge_attr = jax.random.normal(ks[2], (E, EDGE_DIM), jnp.float32)
        msg_w1 = _glorot(ks[3], (2 * H + EDGE_DIM, H))
        msg_b1 = jnp.zeros((H,), jnp.float32)
        msg_w2 = _glorot(ks[4], (H, H))
        msg_b2 = jnp.zeros((H,), jnp.float32)
        msg_w3 = _glorot(ks[5], (H, H))
        msg_b3 = jnp.zeros((H,), jnp.float32)
        upd_w1 = _glorot(ks[6], (2 * H, H))
        upd_b1 = jnp.zeros((H,), jnp.float32)
        upd_w2 = _glorot(ks[7], (H, H))
        upd_b2 = jnp.zeros((H,), jnp.float32)
        upd_w3 = _glorot(ks[8], (H, H))
        upd_b3 = jnp.zeros((H,), jnp.float32)
        ln_g = jnp.ones((H,), jnp.float32)
        ln_b = jnp.zeros((H,), jnp.float32)
        return {'h': h, 'edge_attr': edge_attr, 'msg_w1': msg_w1, 'msg_b1': msg_b1, 'msg_w2': msg_w2, 'msg_b2': msg_b2, 'msg_w3': msg_w3, 'msg_b3': msg_b3, 'upd_w1': upd_w1, 'upd_b1': upd_b1, 'upd_w2': upd_w2, 'upd_b2': upd_b2, 'upd_w3': upd_w3, 'upd_b3': upd_b3, 'ln_g': ln_g, 'ln_b': ln_b, 'edge_index': edge_index}
    _L1_gnn_all = _L1_gnn_setup()
    _L1_gnn_in = {k: v for k, v in _L1_gnn_all.items() if k in ('msg_w1', 'msg_b1', 'msg_w2', 'msg_b2', 'msg_w3', 'msg_b3', 'upd_w1', 'upd_b1', 'upd_w2', 'upd_b2', 'upd_w3', 'upd_b3', 'ln_g', 'ln_b')}
    del _L1_gnn_all
    return {'x': x, 'src': src, 'dst': dst, 'edge_attr_32': edge_attr_32, 'L0_gnn_W1': _L0_gnn_in['W1'], 'L0_gnn_b1': _L0_gnn_in['b1'], 'L0_gnn_W2': _L0_gnn_in['W2'], 'L0_gnn_b2': _L0_gnn_in['b2'], 'L0_gnn_W3': _L0_gnn_in['W3'], 'L0_gnn_b3': _L0_gnn_in['b3'], 'L1_gnn_msg_w1': _L1_gnn_in['msg_w1'], 'L1_gnn_msg_b1': _L1_gnn_in['msg_b1'], 'L1_gnn_msg_w2': _L1_gnn_in['msg_w2'], 'L1_gnn_msg_b2': _L1_gnn_in['msg_b2'], 'L1_gnn_msg_w3': _L1_gnn_in['msg_w3'], 'L1_gnn_msg_b3': _L1_gnn_in['msg_b3'], 'L1_gnn_upd_w1': _L1_gnn_in['upd_w1'], 'L1_gnn_upd_b1': _L1_gnn_in['upd_b1'], 'L1_gnn_upd_w2': _L1_gnn_in['upd_w2'], 'L1_gnn_upd_b2': _L1_gnn_in['upd_b2'], 'L1_gnn_upd_w3': _L1_gnn_in['upd_w3'], 'L1_gnn_upd_b3': _L1_gnn_in['upd_b3'], 'L1_gnn_ln_g': _L1_gnn_in['ln_g'], 'L1_gnn_ln_b': _L1_gnn_in['ln_b']}

def reference(x, src, dst, edge_attr_32, L0_gnn_W1, L0_gnn_b1, L0_gnn_W2, L0_gnn_b2, L0_gnn_W3, L0_gnn_b3, L1_gnn_msg_w1, L1_gnn_msg_b1, L1_gnn_msg_w2, L1_gnn_msg_b2, L1_gnn_msg_w3, L1_gnn_msg_b3, L1_gnn_upd_w1, L1_gnn_upd_b1, L1_gnn_upd_w2, L1_gnn_upd_b2, L1_gnn_upd_w3, L1_gnn_upd_b3, L1_gnn_ln_g, L1_gnn_ln_b):
    import jax
    import jax.numpy as jnp

    def _L0_gnn_ref(x, edge_index, W1, b1, W2, b2, W3, b3):
        import jax, jax.numpy as jnp
        import numpy as np
        N_NODES = 50000
        N_EDGES = 25000
        D_IN = 128
        D_HID = 128
        D_OUT = 128

        def gcn_layer(x, W, b, src, dst, num_nodes):
            h = x @ W
            deg = jnp.zeros((num_nodes,), dtype=h.dtype).at[dst].add(1.0) + 1.0
            dinv = jax.lax.rsqrt(deg)
            coef = dinv[src] * dinv[dst]
            msg = h[src] * coef[:, None]
            agg = jnp.zeros_like(h).at[dst].add(msg)
            agg = agg + h * (dinv * dinv)[:, None]
            return agg + b
        src, dst = (edge_index[0], edge_index[1])
        n = x.shape[0]
        x1 = jax.nn.relu(gcn_layer(x, W1, b1, src, dst, n))
        x2 = jax.nn.relu(gcn_layer(x1, W2, b2, src, dst, n))
        out = gcn_layer(x2, W3, b3, src, dst, n)
        return out

    def _L1_gnn_ref(h, edge_attr, msg_w1, msg_b1, msg_w2, msg_b2, msg_w3, msg_b3, upd_w1, upd_b1, upd_w2, upd_b2, upd_w3, upd_b3, ln_g, ln_b, edge_index):
        import jax, jax.numpy as jnp
        import numpy as np
        N, H, E, EDGE_DIM, STEPS = (50000, 128, 25000, 32, 3)
        LN_EPS = 1e-05

        def _glorot(key, shape):
            fan_in, fan_out = (shape[0], shape[1])
            lim = np.sqrt(6.0 / (fan_in + fan_out)).astype(np.float32)
            return jax.random.uniform(key, shape, jnp.float32, -lim, lim)

        def _mlp(x, w1, b1, w2, b2, w3, b3):
            x = jax.nn.relu(x @ w1 + b1)
            x = jax.nn.relu(x @ w2 + b2)
            return x @ w3 + b3

        def _layernorm(x, g, b):
            mu = jnp.mean(x, axis=-1, keepdims=True)
            var = jnp.mean(jnp.square(x - mu), axis=-1, keepdims=True)
            return (x - mu) * jax.lax.rsqrt(var + LN_EPS) * g + b
        src = edge_index[0]
        dst = edge_index[1]
        n = h.shape[0]
        for _ in range(STEPS):
            m_in = jnp.concatenate([h[src], h[dst], edge_attr], axis=-1)
            m = _mlp(m_in, msg_w1, msg_b1, msg_w2, msg_b2, msg_w3, msg_b3)
            agg = jax.ops.segment_sum(m, dst, num_segments=n)
            upd = _mlp(jnp.concatenate([h, agg], axis=-1), upd_w1, upd_b1, upd_w2, upd_b2, upd_w3, upd_b3)
            h = _layernorm(h + upd, ln_g, ln_b)
        return h
    edge_index = jnp.stack([src, dst])
    h = jnp.maximum(_layernorm(x, axis=-1), 0.0)
    x = x + _L0_gnn_ref(h, edge_index, L0_gnn_W1, L0_gnn_b1, L0_gnn_W2, L0_gnn_b2, L0_gnn_W3, L0_gnn_b3)
    h = jnp.maximum(_layernorm(x, axis=-1), 0.0)
    x = x + _L1_gnn_ref(h, edge_attr_32, L1_gnn_msg_w1, L1_gnn_msg_b1, L1_gnn_msg_w2, L1_gnn_msg_b2, L1_gnn_msg_w3, L1_gnn_msg_b3, L1_gnn_upd_w1, L1_gnn_upd_b1, L1_gnn_upd_w2, L1_gnn_upd_b2, L1_gnn_upd_w3, L1_gnn_upd_b3, L1_gnn_ln_g, L1_gnn_ln_b, edge_index)
    return x

_drawn_inputs = setup_inputs


def setup_inputs(seed=0):
    import zlib

    import numpy as np

    out = dict(_drawn_inputs(seed))
    spreads = {'L0_gnn_b1': (0.0, 0.8),
     'L0_gnn_b2': (0.0, 0.35),
     'L0_gnn_b3': (0.0, 0.1),
     'L1_gnn_msg_b1': (0.0, 0.1),
     'L1_gnn_msg_b2': (0.0, 0.1),
     'L1_gnn_msg_b3': (0.0, 0.1),
     'L1_gnn_upd_b1': (0.0, 0.667),
     'L1_gnn_upd_b2': (0.0, 0.348),
     'L1_gnn_upd_b3': (0.0, 0.284),
     'L1_gnn_ln_g': (1.0, 0.2),
     'L1_gnn_ln_b': (0.0, 0.1)}
    factors = {'L0_gnn_W1': 3.3}
    for name, (base, spread) in spreads.items():
        noise = np.random.default_rng([zlib.crc32(name.encode()), seed]).standard_normal(out[name].shape)
        drawn = base * np.exp(spread * noise) if base else spread * noise
        out[name] = jnp.asarray(drawn.astype(out[name].dtype))
    for name, factor in factors.items():
        out[name] = (out[name] * factor).astype(out[name].dtype)
    return out
```

```python
from contextlib import ExitStack, contextmanager

import concourse.bass as bass
from concourse import mybir

F32 = mybir.dt.float32
BF16 = mybir.dt.bfloat16
I32 = mybir.dt.int32
U32 = mybir.dt.uint32
ALU = mybir.AluOpType
ACT = mybir.ActivationFunctionType
AX = mybir.AxisListType

P = 128
TPC = 4
CHUNK = TPC * P
SLOTS = 4
WIN = 42
EPS = 1e-5


def gnn_program(nc, x, src_pt, dst_pt, dst_flat, edge_t, w_gcn, b_gcn, msg_w, msg_b, upd_w, upd_b, ln_g, ln_b, out):
    N = x.shape[0]
    TILES = src_pt.shape[1]
    CHUNKS = TILES // TPC
    ITERS = CHUNKS // SLOTS
    ED = edge_t.shape[0]
    BLOCKS = -(-N // P)
    NODES = BLOCKS * P
    FULL = N // P
    REST = N - FULL * P
    COLS = NODES + WIN + (WIN & 1)
    GB = TPC
    GROUPS = [(b, min(GB, BLOCKS - b)) for b in range(0, BLOCKS, GB)]
    NG = len(GROUPS)
    MAXPASS = -(-(NODES + 1) // WIN)
    LAYERS = len(w_gcn)
    STEPS = 3

    with ExitStack() as ctx:
        def sb(name, shape, dt=F32):
            return ctx.enter_context(nc.sbuf_tensor(name, shape, dt))

        def sem(name):
            return ctx.enter_context(nc.semaphore(name))

        def cols(b, nb):
            return slice(b * P, (b + nb) * P)

        table = nc.dram_tensor("table", [NODES, P], F32).ap()
        dst_table = nc.dram_tensor("dst_table", [COLS, P], F32).ap()

        bank = [ctx.enter_context(nc.psum_tensor(f"bank{i}", [P, CHUNK], F32)) for i in range(8)]

        wg = sb("wg", [P, LAYERS, P])
        wg_now = sb("wg_now", [P, P])
        bg = sb("bg", [P, LAYERS])
        bg_now = sb("bg_now", [P, 1])
        w1ab = sb("w1ab", [P, 2 * P])
        w1c = sb("w1c", [ED, P])
        w2 = sb("w2", [P, P])
        w3 = sb("w3", [P, P])
        u1a = sb("u1a", [P, P])
        u1b = sb("u1b", [P, P])
        u2 = sb("u2", [P, P])
        u3 = sb("u3", [P, P])
        b1_row = sb("b1_row", [P, P])
        b3_col = sb("b3_col", [P, 1])
        c1_col = sb("c1_col", [P, 1])
        c2_col = sb("c2_col", [P, 1])
        c3_row = sb("c3_row", [P, P])
        g_row = sb("g_row", [P, P])
        be_row = sb("be_row", [P, P])
        b2_rep = sb("b2_rep", [3, P])
        b2_left = sb("b2_left", [3, 2, P])
        b2_part = sb("b2_part", [3, 3, P], BF16)
        b2_split = sb("b2_split", [3, TPC, P], BF16)
        ones_bf = sb("ones_bf", [3, P], BF16)
        ones = sb("ones", [P, P])
        ident = sb("ident", [P, P])
        eps_col = sb("eps_col", [P, 1])
        win_i = sb("win_i", [P, WIN], I32)
        win_iota = sb("win_iota", [P, WIN])
        part_i = sb("part_i", [P, 1], I32)
        part_iota = sb("part_iota", [P, 1])
        step_i = sb("step_i", [P, MAXPASS], I32)
        steps_f = sb("steps_f", [P, MAXPASS])

        src_sb = sb("src_sb", [P, TILES], I32)
        dst_sb = sb("dst_sb", [P, TILES], I32)
        dst_f = sb("dst_f", [P, TILES])
        dst_rows = sb("dst_rows", [CHUNKS, CHUNK], I32)
        lo_hi = sb("lo_hi", [CHUNKS, 2])
        diag = sb("diag", [CHUNKS, 2, CHUNKS])
        lo_all = sb("lo_all", [P, CHUNKS])
        span = sb("span", [P, CHUNKS])
        span_max = sb("span_max", [P, 1])
        over = sb("over", [P, MAXPASS])
        pass_f = sb("pass_f", [P, 1])
        pass_i = sb("pass_i", [P, 1], I32)
        pass_off = sb("pass_off", [P, 1])
        win_lo = sb("win_lo", [P, CHUNKS])
        win_lo_i = sb("win_lo_i", [P, CHUNKS], I32)
        rel = sb("rel", [P, TILES])
        win_node = sb("win_node", [WIN, CHUNKS])

        x_nm = sb("x_nm", [P, BLOCKS, P])
        h_nm = sb("h_nm", [P, BLOCKS, P])
        h_fm = sb("h_fm", [P, NODES])
        agg = sb("agg", [P, COLS])
        deg = sb("deg", [P, COLS])
        dinv = sb("dinv", [P, NODES])
        stage = sb("stage", [P, BLOCKS, P])
        stage2 = sb("stage2", [P, BLOCKS, P])
        stats = sb("stats", [P, BLOCKS, 6])
        mv = sb("mv", [P, BLOCKS, 2])
        rstd = sb("rstd", [P, BLOCKS])
        shift = sb("shift", [P, BLOCKS])

        idx = sb("idx", [P, SLOTS * TPC], I32)
        rows = sb("rows", [P, SLOTS * TPC, P])
        onehot = sb("onehot", [P, SLOTS, TPC, WIN])
        onehot_t = sb("onehot_t", [WIN, SLOTS, CHUNK])
        dst_bc = sb("dst_bc", [WIN, SLOTS, CHUNK], I32)
        dst_win = sb("dst_win", [WIN, SLOTS, P])
        edge_in = sb("edge_in", [ED, SLOTS, CHUNK])
        r1 = sb("r1", [P, 2, CHUNK])
        r2 = sb("r2", [P, SLOTS, CHUNK])
        t1 = sb("t1", [P, 2, CHUNK])
        t2 = sb("t2", [P, 2, CHUNK])

        loaded = sem("loaded")
        first_sem = loaded.num
        loaded_idx = sem("loaded_idx")
        loaded_x = sem("loaded_x")
        pool_done = sem("pool_done")
        dve_done = sem("dve_done")
        act_done = sem("act_done")
        pe_done = sem("pe_done")
        pe2_done = sem("pe2_done")
        pe3_done = sem("pe3_done")
        stored = sem("stored")
        idx_ready = sem("idx_ready")
        onehot_ready = sem("onehot_ready")
        onehot_t_ready = sem("onehot_t_ready")
        seg_done = sem("seg_done")
        window_added = sem("window_added")
        z_done = sem("z_done")
        gathers_begun = sem("gathers_begun")
        relu1_done = sem("relu1_done")
        y_done = sem("y_done")
        relu2_done = sem("relu2_done")
        dst_bc_in = [sem(f"dst_bc_in{k}") for k in range(SLOTS)]
        dst_win_in = [sem(f"dst_win_in{k}") for k in range(SLOTS)]
        edge_in_in = [sem(f"edge_in_in{k}") for k in range(SLOTS)]
        gathered = [sem(f"gathered{j}") for j in range(SLOTS * TPC)]
        all_sems = [loaded, loaded_idx, loaded_x, pool_done, dve_done, act_done, pe_done, pe2_done, pe3_done, stored,
                    idx_ready, onehot_ready, onehot_t_ready, seg_done, window_added, gathers_begun, z_done, relu1_done, y_done,
                    relu2_done, *dst_bc_in, *dst_win_in, *edge_in_in, *gathered]
        nums = sorted(s.num for s in all_sems)
        assert nums == list(range(nums[0], nums[-1] + 1))
        gathers = sorted(s.num for s in gathered)

        @contextmanager
        def phase(name, gather=False):
            with nc.Block(name) as block:
                yield block
            if gather:
                nc.gpsimd.dma_reset(range(gathers[0], gathers[-1] + 1))
            nc.all_engine_barrier(sems_to_clear=range(nums[0], nums[-1] + 1))

        class Chain:

            def __init__(self, eng, s):
                self.eng, self.s, self.n = eng, s, 0

            def __call__(self, ins):
                self.n += 1
                ins.then_inc(self.s, 1)
                self.eng.wait_ge(self.s, self.n)

        with phase("load") as block:
            @block.sync
            def _(sp):
                sp.dma_start(dst_rows[:, :], dst_flat.rearrange("(c e) -> c e", e=CHUNK)).then_inc(loaded_idx, 16)
                sp.dma_start(dst_sb[:, :], dst_pt).then_inc(loaded_idx, 16)
                sp.dma_start(src_sb[:, :], src_pt).then_inc(loaded_idx, 16)
                sp.wait_ge(pool_done, 1)
                sp.dma_start(x_nm[:, 0:FULL, :], x[0:FULL * P, :].rearrange("(b p) f -> p b f", p=P)).then_inc(loaded_x, 16)
                sp.dma_start(x_nm[0:REST, FULL, :], x[FULL * P:N, :]).then_inc(loaded_x, 16)
                sp.wait_ge(loaded_x, 32)
                sp.wait_ge(pool_done, 2)
                sp.dma_start(dst_table[NODES:COLS, :], ones[0:COLS - NODES, :]).then_inc(stored, 16)
                sp.wait_ge(stored, 16)

            @block.scalar
            def _(act):
                def col(v):
                    return v.rearrange("(p o) -> p o", o=1)

                def row(v, n):
                    return v.rearrange("(o f) -> o f", o=1).to_broadcast([n, P])

                small = [(wg[:, l, :], w_gcn[l]) for l in range(LAYERS)]
                small += [(bg[:, l:l + 1], col(b_gcn[l])) for l in range(LAYERS)]
                small += [(w1ab[:, 0:P], msg_w[0][0:P, :]), (w1ab[:, P:2 * P], msg_w[0][P:2 * P, :]),
                          (w1c[:, :], msg_w[0][2 * P:2 * P + ED, :]), (w2[:, :], msg_w[1]), (w3[:, :], msg_w[2]),
                          (u1a[:, :], upd_w[0][0:P, :]), (u1b[:, :], upd_w[0][P:2 * P, :]), (u2[:, :], upd_w[1]),
                          (u3[:, :], upd_w[2]), (b1_row[:, :], row(msg_b[0], P)), (b2_rep[:, :], row(msg_b[1], 3)),
                          (b3_col[:, :], col(msg_b[2])), (c1_col[:, :], col(upd_b[0])), (c2_col[:, :], col(upd_b[1])),
                          (c3_row[:, :], row(upd_b[2], P)), (g_row[:, :], row(ln_g, P)), (be_row[:, :], row(ln_b, P))]
                for to, frm in small:
                    act.dma_start(to, frm).then_inc(loaded, 16)
                act.wait_ge(loaded, 16 * len(small))
                act.sem_inc(act_done, 1)

            @block.gpsimd
            def _(pool):
                pool.memset(x_nm[:, FULL:BLOCKS, :], 0.0).then_inc(pool_done, 1)
                pool.memset(ones[:, :], 1.0).then_inc(pool_done, 1)
                pool.memset(ident[:, :], 0.0).then_inc(pool_done, 1)
                pool.wait_ge(pool_done, 3)
                pool.affine_select(out=ident[:, :], in_=ident[:, :], compare_op=ALU.not_equal, fill=1.0,
                                   base=0, pattern=[[-1, P]], channel_multiplier=1).then_inc(pool_done, 1)
                pool.iota(win_i[:, :], pattern=[[1, WIN]], base=0, channel_multiplier=0).then_inc(pool_done, 1)
                pool.iota(part_i[:, :], pattern=[[0, 1]], base=0, channel_multiplier=1).then_inc(pool_done, 1)
                pool.iota(step_i[:, :], pattern=[[WIN, MAXPASS]], base=0, channel_multiplier=0).then_inc(pool_done, 1)
                pool.memset(eps_col[:, :], EPS)
                pool.memset(ones_bf[:, :], 1.0)
                pool.memset(agg[:, :], 0.0)
                pool.memset(deg[:, :], 0.0)

            @block.vector
            def _(dve):
                link = Chain(dve, dve_done)
                dve.wait_ge(loaded_idx, 48)
                dve.tensor_copy(dst_f[:, :], dst_sb[:, :])
                dve.tensor_reduce(lo_hi[:, 0:1], dst_rows[:, :], AX.X, ALU.min)
                link(dve.tensor_reduce(lo_hi[:, 1:2], dst_rows[:, :], AX.X, ALU.max))
                dve.wait_ge(pool_done, 7)
                dve.tensor_scalar(diag[:, 0, :], ident[0:CHUNKS, 0:CHUNKS], lo_hi[:, 0:1], None, ALU.mult)
                dve.tensor_scalar(diag[:, 1, :], ident[0:CHUNKS, 0:CHUNKS], lo_hi[:, 1:2], None, ALU.mult).then_inc(z_done, 1)
                dve.tensor_copy(win_iota[:, :], win_i[:, :])
                dve.tensor_copy(part_iota[:, :], part_i[:, :])
                link(dve.tensor_copy(steps_f[:, :], step_i[:, :]))
                dve.wait_ge(pe_done, 1)
                link(dve.tensor_copy(lo_all[:, :], bank[0][:, 0:CHUNKS]))
                link(dve.tensor_tensor(span[:, :], bank[0][:, CHUNKS:2 * CHUNKS], lo_all[:, :], ALU.subtract))
                link(dve.tensor_reduce(span_max[:, :], span[:, :], AX.X, ALU.max))
                link(dve.tensor_scalar(over[:, :], steps_f[:, :], span_max[:, 0:1], None, ALU.is_le))
                link(dve.tensor_reduce(pass_f[:, :], over[:, :], AX.X, ALU.add))
                link(dve.tensor_copy(pass_i[:, :], pass_f[:, :]))
                dve.wait_ge(act_done, 1)
                link(dve.tensor_copy(b2_part[:, 0, :], b2_rep[:, :]))
                link(dve.tensor_tensor(b2_left[:, 0, :], b2_rep[:, :], b2_part[:, 0, :], ALU.subtract))
                link(dve.tensor_copy(b2_part[:, 1, :], b2_left[:, 0, :]))
                link(dve.tensor_tensor(b2_left[:, 1, :], b2_left[:, 0, :], b2_part[:, 1, :], ALU.subtract))
                link(dve.tensor_copy(b2_part[:, 2, :], b2_left[:, 1, :]))
                for s in range(3):
                    link(dve.tensor_scalar(b2_left[:, s % 2, :], b2_part[:, s, :], ident[0:3, s:s + 1], None, ALU.mult)
                         if s == 0 else
                         dve.scalar_tensor_tensor(out=b2_left[:, s % 2, :], in0=b2_part[:, s, :], scalar=ident[0:3, s:s + 1],
                                                  in1=b2_left[:, (s + 1) % 2, :], op0=ALU.mult, op1=ALU.add))
                for t in range(TPC):
                    dve.tensor_copy(b2_split[:, t, :], b2_left[:, 0, :])

            @block.tensor
            def _(pe):
                pe.wait_ge(z_done, 1)
                pe.matmul(bank[0][:, 0:2 * CHUNKS], ones[0:CHUNKS, :], diag[:, :, :].rearrange("p a c -> p (a c)"),
                          start=True, stop=True).then_inc(pe_done, 1)

        passes = nc.values_load(pass_i[0:1, 0:1], min_val=1, max_val=MAXPASS)

        def edge_passes(name, target, rows_of, messages):
            with phase(f"{name}_start") as block:
                @block.vector
                def _(dve):
                    dve.memset(pass_off[:, :], 0.0)

            with nc.Fori(0, passes):
                with phase(f"{name}_windows") as block:
                    @block.vector
                    def _(dve):
                        link = Chain(dve, dve_done)
                        link(dve.tensor_scalar(win_lo[:, :], lo_all[:, :], pass_off[:, 0:1], float(NODES), ALU.add, ALU.min))
                        dve.tensor_copy(win_lo_i[:, :], win_lo[:, :])
                        dve.tensor_scalar(win_node[:, :], win_lo[0:WIN, :], part_iota[0:WIN, 0:1], None, ALU.add)
                        dve.tensor_tensor(rel[:, :].rearrange("p (c t) -> p c t", t=TPC),
                                          dst_f[:, :].rearrange("p (c t) -> p c t", t=TPC),
                                          win_lo[:, :].unsqueeze(2).to_broadcast([P, CHUNKS, TPC]), ALU.subtract)
                        dve.tensor_scalar(pass_off[:, :], pass_off[:, :], float(WIN), None, ALU.add)

                with phase(f"{name}_edges", gather=rows_of is not None) as block:
                    edge_engines(block, target, rows_of, messages)

        def edge_engines(block, target, rows_of, messages):
            z = [bank[0], bank[1]]
            y = [bank[2], bank[3]]
            acc = [bank[4], bank[5]]

            @block.vector
            def _(dve):
                def prepare(i, k):
                    dve.wait_ge(seg_done, i * SLOTS + k + 1)
                    if rows_of is not None:
                        dve.tensor_copy(idx[:, k * TPC:(k + 1) * TPC],
                                        src_sb[:, bass.ds((i * SLOTS + k) * TPC, TPC)]).then_inc(idx_ready, 1)
                    dve.tensor_tensor(
                        onehot[:, k, :, :],
                        rel[:, bass.ds((i * SLOTS + k) * TPC, TPC)].unsqueeze(2).to_broadcast([P, TPC, WIN]),
                        win_iota[:, :].unsqueeze(1).to_broadcast([P, TPC, WIN]),
                        ALU.is_equal).then_inc(onehot_ready, 1)
                    if messages:
                        dve.wait_ge(dst_bc_in[k], 16 * (i + 1))
                        dve.tensor_scalar(onehot_t[:, k, :], dst_bc[:, k, :], win_node[:, bass.ds(i * SLOTS + k, 1)],
                                          None, ALU.is_equal).then_inc(onehot_t_ready, 1)

                def add_window(i, k):
                    at = dve.value_load(win_lo_i[0:1, bass.ds(i * SLOTS + k, 1)], min_val=0, max_val=NODES)
                    dve.wait_ge(seg_done, i * SLOTS + k + 1 + SLOTS)
                    dve.wait_ge(window_added, i * SLOTS + k + 2)
                    w = target[:, bass.ds(at, WIN)]
                    dve.tensor_tensor(w, w, acc[k % 2][:, 0:WIN], ALU.add).then_inc(window_added, 1)

                for k in range(SLOTS):
                    prepare(0, k)
                with dve.Fori(0, ITERS - 1) as i:
                    for k in range(SLOTS):
                        add_window(i, k)
                        prepare(i + 1, k)
                for k in range(SLOTS):
                    add_window(ITERS - 1, k)

            @block.gpsimd
            def _(pool):
                if rows_of is None:
                    return
                with pool.Fori(0, ITERS) as i:
                    for k in range(SLOTS):
                        pool.wait_ge(idx_ready, i * SLOTS + k + 1)
                        pool.sem_inc(gathers_begun, 1)
                        for j in range(k * TPC, (k + 1) * TPC):
                            pool.indirect_dma_start(
                                out=rows[:, j, :], out_offset=None, in_=rows_of,
                                in_offset=bass.IndirectOffsetOnAxis(ap=idx[:, j:j + 1].bitcast(U32), axis=0),
                            ).then_inc(gathered[j], 16)

            @block.sync
            def _(sp):
                if not messages:
                    return
                with sp.Fori(0, ITERS) as i:
                    for k in range(SLOTS):
                        c = i * SLOTS + k
                        at = sp.value_load(win_lo_i[0:1, bass.ds(c, 1)], min_val=0, max_val=NODES)
                        sp.wait_ge(z_done, c + 1)
                        sp.dma_start(dst_bc[:, k, :],
                                     dst_flat[bass.ds(c * CHUNK, CHUNK)].rearrange("(o e) -> o e", o=1).to_broadcast([WIN, CHUNK])
                                     ).then_inc(dst_bc_in[k], 16)
                        sp.dma_start(edge_in[:, k, :], edge_t[:, bass.ds(c * CHUNK, CHUNK)]).then_inc(edge_in_in[k], 16)
                        sp.dma_start(dst_win[:, k, :], dst_table[bass.ds(at, WIN), :]).then_inc(dst_win_in[k], 16)

            @block.scalar
            def _(act):
                if not messages:
                    return

                def relu1(i, k):
                    act.wait_ge(z_done, i * SLOTS + k + 1 + SLOTS)
                    act.wait_ge(y_done, i * SLOTS + k + 1)
                    act.activation(r1[:, k % 2, :], z[k % 2][:, :], ACT.Relu).then_inc(relu1_done, 1)

                def relu2(i, k):
                    act.wait_ge(y_done, i * SLOTS + k + 1 + 2)
                    act.wait_ge(seg_done, i * SLOTS + k + 1)
                    act.activation(r2[:, k, :], y[k % 2][:, :], ACT.Relu).then_inc(relu2_done, 1)

                with act.Fori(0, ITERS) as i:
                    for k in range(SLOTS + 1):
                        if k < SLOTS:
                            relu1(i, k)
                        if k >= 1:
                            relu2(i, k - 1)

            @block.tensor
            def _(pe):
                pe.sem_inc(seg_done, SLOTS)
                pe.sem_inc(window_added, 2)
                if messages:
                    pe.sem_inc(z_done, SLOTS)
                    pe.sem_inc(relu1_done, 2)
                    pe.sem_inc(y_done, 2)
                    pe.sem_inc(relu2_done, 2)

                def first(i, k):
                    c = i * SLOTS + k
                    pe.wait_ge(relu1_done, c + 1)
                    pe.wait_ge(edge_in_in[k], 16 * (i + 1))
                    pe.matmul(z[k % 2][:, :], w1c[:, :], edge_in[:, k, :], start=True, stop=False)
                    pe.wait_ge(dst_win_in[k], 16 * (i + 1))
                    pe.wait_ge(onehot_t_ready, c + 1)
                    pe.matmul(z[k % 2][:, :], dst_win[:, k, :], onehot_t[:, k, :], start=False, stop=False)
                    for t in range(TPC):
                        pe.wait_ge(gathered[k * TPC + t], 16 * (i + 1))
                        last = pe.matmul(z[k % 2][:, t * P:(t + 1) * P], rows[:, k * TPC + t, :], ident[:, :],
                                         start=False, stop=(t == TPC - 1))
                    last.then_inc(z_done, 1)

                def second(i, k):
                    c = i * SLOTS + k
                    pe.wait_ge(relu2_done, c + 1)
                    pe.matmul(y[k % 2][:, :], ones_bf[:, :], b2_split[:, :, :].rearrange("p t f -> p (t f)"),
                              start=True, stop=False)
                    pe.wait_ge(relu1_done, c + 1 + 2)
                    for t in range(TPC):
                        last = pe.matmul(y[k % 2][:, t * P:(t + 1) * P], r1[:, k % 2, t * P:(t + 1) * P], w2[:, :],
                                         start=False, stop=(t == TPC - 1))
                    last.then_inc(y_done, 1)

                def summed(i, k):
                    c = i * SLOTS + k
                    pe.wait_ge(onehot_ready, c + 1)
                    pe.wait_ge(window_added, c + 1)
                    if messages:
                        pe.wait_ge(relu2_done, c + 1 + 2)
                    for t in range(TPC):
                        if messages:
                            what = r2[:, k, t * P:(t + 1) * P]
                        elif rows_of is not None:
                            pe.wait_ge(gathered[k * TPC + t], 16 * (i + 1))
                            what = rows[:, k * TPC + t, :]
                        else:
                            what = ones[:, :]
                        last = pe.matmul(acc[k % 2][:, 0:WIN], what, onehot[:, k, t, :],
                                         start=(t == 0), stop=(t == TPC - 1))
                    last.then_inc(seg_done, 1)

                with pe.Fori(0, ITERS) as i:
                    for k in range(SLOTS + 2):
                        if messages and k < SLOTS:
                            first(i, k)
                        if messages and 1 <= k <= SLOTS:
                            second(i, k - 1)
                        if k >= 2:
                            summed(i, k - 2)

        edge_passes("degree", deg, None, False)

        def norm_dve(dve, link, frm):
            for b in range(BLOCKS):
                ins = dve.bn_stats(stats[:, b, :], frm[:, b, :])
            link(ins)
            for b in range(BLOCKS):
                ins = dve.bn_aggr(mv[:, b, :], stats[:, b, :])
            ins.then_inc(z_done, 1)
            dve.wait_ge(y_done, 1)
            link(dve.reciprocal(rstd[:, :], rstd[:, :]))
            dve.scalar_tensor_tensor(out=shift[:, :], in0=mv[:, :, 0], scalar=-1.0, in1=rstd[:, :],
                                     op0=ALU.mult, op1=ALU.mult).then_inc(relu1_done, 1)

        def norm_act(act, frm, to, func):
            act.wait_ge(z_done, 1)
            act.activation(rstd[:, :], mv[:, :, 1], ACT.Sqrt, bias=eps_col[:, 0:1]).then_inc(y_done, 1)
            act.wait_ge(relu1_done, 1)
            for b, nb in GROUPS:
                for t in range(b, b + nb):
                    ins = act.activation(to[:, t, :], frm[:, t, :], func, bias=shift[:, t:t + 1], scale=rstd[:, t:t + 1])
                ins.then_inc(relu2_done, 1)

        with phase("gcn_input") as block:
            @block.vector
            def _(dve):
                link = Chain(dve, dve_done)
                norm_dve(dve, link, x_nm)
                dve.wait_ge(act_done, 1)
                link(dve.reciprocal(dinv[:, :], dinv[:, :]))
                for n, (b, nb) in enumerate(GROUPS):
                    dve.wait_ge(pe_done, n + 1)
                    dve.tensor_tensor(h_fm[:, cols(b, nb)], bank[n][:, 0:nb * P], dinv[:, cols(b, nb)], ALU.mult)

            @block.scalar
            def _(act):
                act.activation(dinv[:, :], deg[:, 0:NODES], ACT.Sqrt, bias=1.0).then_inc(act_done, 1)
                norm_act(act, x_nm, h_nm, ACT.Relu)

            @block.tensor
            def _(pe):
                for n, (b, nb) in enumerate(GROUPS):
                    pe.wait_ge(relu2_done, n + 1)
                    for t in range(nb):
                        last = pe.transpose(bank[n][:, t * P:(t + 1) * P], h_nm[:, b + t, :], ident[:, :])
                    last.then_inc(pe_done, 1)

        with nc.Fori(0, LAYERS) as layer:
            with phase("gcn_table") as block:
                @block.scalar
                def _(act):
                    act.activation(wg_now[:, :], wg[:, bass.ds(layer, 1), :].rearrange("p o f -> p (o f)"), ACT.Copy).then_inc(act_done, 1)
                    act.activation(bg_now[:, :], bg[:, bass.ds(layer, 1)], ACT.Copy)
                    for n, (b, nb) in enumerate(GROUPS):
                        act.wait_ge(pe_done, n + 1)
                        act.activation(stage[:, b:b + nb, :].rearrange("p b f -> p (b f)"), bank[n % 4][:, 0:nb * P],
                                       ACT.Copy).then_inc(relu1_done, 1)

                @block.tensor
                def _(pe):
                    pe.wait_ge(act_done, 1)
                    for n, (b, nb) in enumerate(GROUPS):
                        if n >= 4:
                            pe.wait_ge(relu1_done, n - 3)
                        for t in range(nb):
                            last = pe.matmul(bank[n % 4][:, t * P:(t + 1) * P], h_fm[:, cols(b + t, 1)], wg_now[:, :],
                                             start=True, stop=True)
                        last.then_inc(pe_done, 1)
                        if n >= 4:
                            pe.wait_ge(dve_done, n - 3)
                        pe.matmul(bank[4 + n % 4][:, 0:nb * P], wg_now[:, :], h_fm[:, cols(b, nb)],
                                  start=True, stop=True).then_inc(pe2_done, 1)

                @block.vector
                def _(dve):
                    for n, (b, nb) in enumerate(GROUPS):
                        dve.wait_ge(pe2_done, n + 1)
                        dve.tensor_copy(agg[:, cols(b, nb)], bank[4 + n % 4][:, 0:nb * P]).then_inc(dve_done, 1)

                @block.sync
                def _(sp):
                    for n, (b, nb) in enumerate(GROUPS):
                        sp.wait_ge(relu1_done, n + 1)
                        sp.dma_start(table[cols(b, nb), :].rearrange("(b p) f -> p b f", p=P),
                                     stage[:, b:b + nb, :]).then_inc(stored, 16)
                    sp.wait_ge(stored, 16 * NG)

            edge_passes("gcn", agg, table, False)

            with phase("gcn_act") as block:
                @block.vector
                def _(dve):
                    for n, (b, nb) in enumerate(GROUPS):
                        dve.tensor_tensor(agg[:, cols(b, nb)], agg[:, cols(b, nb)], dinv[:, cols(b, nb)],
                                          ALU.mult).then_inc(dve_done, 1)
                    for n, (b, nb) in enumerate(GROUPS):
                        dve.wait_ge(act_done, n + 1)
                        dve.tensor_tensor(h_fm[:, cols(b, nb)], h_fm[:, cols(b, nb)], dinv[:, cols(b, nb)], ALU.mult)

                @block.scalar
                def _(act):
                    for n, (b, nb) in enumerate(GROUPS):
                        act.wait_ge(dve_done, n + 1)
                        act.activation(h_fm[:, cols(b, nb)], agg[:, cols(b, nb)], ACT.Relu,
                                       bias=bg_now[:, 0:1]).then_inc(act_done, 1)

        def to_feature_major(pe):
            for n, (b, nb) in enumerate(GROUPS):
                pe.wait_ge(relu2_done, n + 1)
                for t in range(nb):
                    last = pe.transpose(bank[n][:, t * P:(t + 1) * P], h_nm[:, b + t, :], ident[:, :])
                last.then_inc(pe2_done, 1)

        with phase("gcn_out") as block:
            @block.scalar
            def _(act):
                for n, (b, nb) in enumerate(GROUPS):
                    act.activation(agg[:, cols(b, nb)], agg[:, cols(b, nb)], ACT.Identity,
                                   bias=bg_now[:, 0:1]).then_inc(act_done, 1)
                norm_act(act, x_nm, h_nm, ACT.Relu)

            @block.tensor
            def _(pe):
                for n, (b, nb) in enumerate(GROUPS):
                    pe.wait_ge(act_done, n + 1)
                    for t in range(nb):
                        last = pe.transpose(bank[n][:, t * P:(t + 1) * P], agg[:, cols(b + t, 1)], ident[:, :])
                    last.then_inc(pe_done, 1)
                pe.wait_ge(pe3_done, 1)
                to_feature_major(pe)

            @block.vector
            def _(dve):
                link = Chain(dve, dve_done)
                for n, (b, nb) in enumerate(GROUPS):
                    dve.wait_ge(pe_done, n + 1)
                    ins = dve.tensor_tensor(x_nm[:, b:b + nb, :].rearrange("p b f -> p (b f)"),
                                            x_nm[:, b:b + nb, :].rearrange("p b f -> p (b f)"), bank[n][:, 0:nb * P], ALU.add)
                link(ins)
                dve.sem_inc(pe3_done, 1)
                norm_dve(dve, link, x_nm)
                for n, (b, nb) in enumerate(GROUPS):
                    dve.wait_ge(pe2_done, n + 1)
                    dve.tensor_copy(h_fm[:, cols(b, nb)], bank[n][:, 0:nb * P])

        with nc.Fori(0, STEPS) as _step:
            with phase("mp_table") as block:
                @block.gpsimd
                def _(pool):
                    pool.memset(agg[:, :], 0.0)

                @block.tensor
                def _(pe):
                    for n, (b, nb) in enumerate(GROUPS):
                        for half, read in ((0, relu1_done), (1, relu2_done)):
                            if n >= 4:
                                pe.wait_ge(read, n - 3)
                            for t in range(nb):
                                last = pe.matmul(bank[4 * half + n % 4][:, t * P:(t + 1) * P], h_fm[:, cols(b + t, 1)],
                                                 w1ab[:, half * P:(half + 1) * P], start=True, stop=True)
                            last.then_inc(pe_done, 1)

                @block.scalar
                def _(act):
                    for n, (b, nb) in enumerate(GROUPS):
                        act.wait_ge(pe_done, 2 * n + 1)
                        act.activation(stage[:, b:b + nb, :].rearrange("p b f -> p (b f)"), bank[n % 4][:, 0:nb * P],
                                       ACT.Copy).then_inc(relu1_done, 1)

                @block.vector
                def _(dve):
                    for n, (b, nb) in enumerate(GROUPS):
                        dve.wait_ge(pe_done, 2 * n + 2)
                        dve.tensor_tensor(stage2[:, b:b + nb, :],
                                          bank[4 + n % 4][:, 0:nb * P].rearrange("p (b f) -> p b f", f=P),
                                          b1_row[:, :].unsqueeze(1).to_broadcast([P, nb, P]), ALU.add).then_inc(relu2_done, 1)

                @block.sync
                def _(sp):
                    for n, (b, nb) in enumerate(GROUPS):
                        for s, ready, to in ((stage, relu1_done, table), (stage2, relu2_done, dst_table)):
                            sp.wait_ge(ready, n + 1)
                            sp.dma_start(to[cols(b, nb), :].rearrange("(b p) f -> p b f", p=P),
                                         s[:, b:b + nb, :]).then_inc(stored, 16)
                    sp.wait_ge(stored, 32 * NG)

            edge_passes("mp", agg, table, True)

            with phase("update") as block:
                @block.tensor
                def _(pe):
                    for n, (b, nb) in enumerate(GROUPS):
                        c = nb * P
                        if n >= 1:
                            pe.wait_ge(dve_done, 2 * n)
                            pe.wait_ge(act_done, 2 * n)
                        pe.matmul(bank[0][:, 0:c], w3[:, :], agg[:, cols(b, nb)], start=True, stop=True).then_inc(pe_done, 1)
                        pe.matmul(bank[1][:, 0:c], u1a[:, :], h_fm[:, cols(b, nb)], start=True, stop=False)
                        pe.wait_ge(dve_done, 2 * n + 1)
                        pe.matmul(bank[1][:, 0:c], u1b[:, :], t1[:, 0, 0:c], start=False, stop=True).then_inc(pe_done, 1)
                        pe.wait_ge(act_done, 2 * n + 1)
                        pe.matmul(bank[2][:, 0:c], u2[:, :], t2[:, 0, 0:c], start=True, stop=True).then_inc(pe_done, 1)
                        pe.wait_ge(act_done, 2 * n + 2)
                        for t in range(nb):
                            last = pe.matmul(bank[3][:, t * P:(t + 1) * P], t2[:, 1, t * P:(t + 1) * P], u3[:, :],
                                             start=True, stop=True)
                        last.then_inc(pe_done, 1)
                    pe.wait_ge(dve_done, 2 * NG)
                    to_feature_major(pe)

                @block.vector
                def _(dve):
                    for n, (b, nb) in enumerate(GROUPS):
                        c = nb * P
                        dve.wait_ge(pe_done, 4 * n + 1)
                        dve.scalar_tensor_tensor(out=t1[:, 0, 0:c], in0=deg[:, cols(b, nb)], scalar=b3_col[:, 0:1],
                                                 in1=bank[0][:, 0:c], op0=ALU.mult, op1=ALU.add).then_inc(dve_done, 1)
                        dve.tensor_tensor(h_nm[:, b:b + nb, :], h_nm[:, b:b + nb, :],
                                          c3_row[:, :].unsqueeze(1).to_broadcast([P, nb, P]), ALU.add).then_inc(onehot_ready, 1)
                        dve.wait_ge(onehot_ready, n + 1)
                        dve.wait_ge(pe_done, 4 * n + 4)
                        h2 = h_nm[:, b:b + nb, :].rearrange("p b f -> p (b f)")
                        dve.tensor_tensor(h2, h2, bank[3][:, 0:c], ALU.add).then_inc(dve_done, 1)
                    dve.wait_ge(dve_done, 2 * NG)
                    link = Chain(dve, seg_done)
                    norm_dve(dve, link, h_nm)
                    for n, (b, nb) in enumerate(GROUPS):
                        dve.wait_ge(onehot_t_ready, n + 1)
                        h3 = h_nm[:, b:b + nb, :]
                        link(dve.tensor_tensor(h3, h3, g_row[:, :].unsqueeze(1).to_broadcast([P, nb, P]), ALU.mult))
                        dve.tensor_tensor(h3, h3, be_row[:, :].unsqueeze(1).to_broadcast([P, nb, P]), ALU.add).then_inc(relu2_done, 1)
                    for n, (b, nb) in enumerate(GROUPS):
                        dve.wait_ge(pe2_done, n + 1)
                        dve.tensor_copy(h_fm[:, cols(b, nb)], bank[n][:, 0:nb * P])

                @block.scalar
                def _(act):
                    for n, (b, nb) in enumerate(GROUPS):
                        c = nb * P
                        act.wait_ge(pe_done, 4 * n + 2)
                        act.activation(t2[:, 0, 0:c], bank[1][:, 0:c], ACT.Relu, bias=c1_col[:, 0:1]).then_inc(act_done, 1)
                        act.wait_ge(pe_done, 4 * n + 3)
                        act.activation(t2[:, 1, 0:c], bank[2][:, 0:c], ACT.Relu, bias=c2_col[:, 0:1]).then_inc(act_done, 1)
                    act.wait_ge(z_done, 1)
                    act.activation(rstd[:, :], mv[:, :, 1], ACT.Sqrt, bias=eps_col[:, 0:1]).then_inc(y_done, 1)
                    act.wait_ge(relu1_done, 1)
                    for b, nb in GROUPS:
                        for t in range(b, b + nb):
                            ins = act.activation(h_nm[:, t, :], h_nm[:, t, :], ACT.Identity, bias=shift[:, t:t + 1],
                                                 scale=rstd[:, t:t + 1])
                        ins.then_inc(onehot_t_ready, 1)

        with phase("output") as block:
            @block.vector
            def _(dve):
                dve.tensor_tensor(x_nm[:, :, :], x_nm[:, :, :], h_nm[:, :, :], ALU.add).then_inc(dve_done, 1)

            @block.sync
            def _(sp):
                sp.wait_ge(dve_done, 1)
                sp.dma_start(out[0:FULL * P, :].rearrange("(b p) f -> p b f", p=P), x_nm[:, 0:FULL, :]).then_inc(stored, 16)
                sp.dma_start(out[FULL * P:N, :], x_nm[0:REST, FULL, :]).then_inc(stored, 16)
                sp.wait_ge(stored, 32)


def kernel(**inputs):
    import numpy as np
    import concourse.bacc as bacc
    from concourse.bass_utils import run_bass_kernel_spmd

    a = {k: np.asarray(v) for k, v in inputs.items()}
    n, d = a["x"].shape
    edges = a["src"].shape[0]
    group = SLOTS * CHUNK
    padded = -(-edges // group) * group
    src = np.zeros(padded, a["src"].dtype)
    src[:edges] = a["src"]
    dst = np.full(padded, n, a["dst"].dtype)
    dst[:edges] = a["dst"]
    edge_t = np.zeros((a["edge_attr_32"].shape[1], padded), a["edge_attr_32"].dtype)
    edge_t[:, :edges] = a["edge_attr_32"].T
    arrays = {
        "x": a["x"],
        "src_pt": np.ascontiguousarray(src.reshape(-1, P).T),
        "dst_pt": np.ascontiguousarray(dst.reshape(-1, P).T),
        "dst_flat": dst,
        "edge_t": edge_t,
    }
    groups = {
        "w_gcn": [f"L0_gnn_W{i}" for i in (1, 2, 3)], "b_gcn": [f"L0_gnn_b{i}" for i in (1, 2, 3)],
        "msg_w": [f"L1_gnn_msg_w{i}" for i in (1, 2, 3)], "msg_b": [f"L1_gnn_msg_b{i}" for i in (1, 2, 3)],
        "upd_w": [f"L1_gnn_upd_w{i}" for i in (1, 2, 3)], "upd_b": [f"L1_gnn_upd_b{i}" for i in (1, 2, 3)],
    }
    for names in groups.values():
        arrays |= {name: a[name] for name in names}
    arrays |= {"ln_g": a["L1_gnn_ln_g"], "ln_b": a["L1_gnn_ln_b"]}

    nc = bacc.Bacc("TRN2", target_bir_lowering=False, num_devices=1)
    aps = {k: nc.dram_tensor(f"in_{k}", v.shape, mybir.dt.from_np(v.dtype), kind="ExternalInput").ap()
           for k, v in arrays.items()}
    out = nc.dram_tensor("out", (n, d), F32, kind="ExternalOutput").ap()
    gnn_program(nc, aps["x"], aps["src_pt"], aps["dst_pt"], aps["dst_flat"], aps["edge_t"],
                *([aps[name] for name in names] for names in groups.values()), aps["ln_g"], aps["ln_b"], out)
    r = run_bass_kernel_spmd(nc, [{f"in_{k}": v for k, v in arrays.items()}], core_ids=[0])
    return r.results[0]["out"]
```

```python
from contextlib import ExitStack, contextmanager

import concourse.bass as bass
from concourse import mybir

F32 = mybir.dt.float32
BF16 = mybir.dt.bfloat16
I16 = mybir.dt.int16
U8 = mybir.dt.uint8
I32 = mybir.dt.int32
U32 = mybir.dt.uint32
ALU = mybir.AluOpType
ACT = mybir.ActivationFunctionType
AX = mybir.AxisListType

P = 128
TPC = 4
CHUNK = TPC * P
SLOTS = 4
WIN = 39
CWIN = 44
DENSE_MAX = 120
EPS = 1e-5


def gnn_program(nc, x, src_pt, dst_pt, dst_flat, edge_q, w_gcn, b_gcn, msg_w, msg_b, upd_w, upd_b, ln_g, ln_b, out):
    N = x.shape[0]
    TILES = src_pt.shape[1]
    CHUNKS = TILES // TPC
    ITERS = CHUNKS // SLOTS
    QUARTERS = 4
    ED = P // QUARTERS
    QCOLS = edge_q.shape[1]
    SPLIT = 1024
    BLOCKS = -(-N // P)
    NODES = BLOCKS * P
    FULL = N // P
    REST = N - FULL * P
    COLS = NODES + CWIN
    GB = TPC
    GROUPS = [(b, min(GB, BLOCKS - b)) for b in range(0, BLOCKS, GB)]
    NG = len(GROUPS)
    MAXPASS = -(-(NODES + 1) // WIN)
    LAYERS = len(w_gcn)
    STEPS = 3
    TB = -(-BLOCKS // 3)
    THIRDS = [(b, min(TB, BLOCKS - b)) for b in range(0, BLOCKS, TB)]
    KEYS = BLOCKS * CWIN
    assert TB * CWIN <= CHUNK and COLS % 4 == 0 and CWIN % 4 == 0 and CWIN >= WIN + 3
    ROUNDS = QCOLS // SPLIT
    LAYER_STEP = -(-(ROUNDS - 1) // LAYERS)
    assert QCOLS % SPLIT == 0 and LAYER_STEP * LAYERS + 1 == ROUNDS

    with ExitStack() as ctx:
        def sb(name, shape, dt=F32):
            return ctx.enter_context(nc.sbuf_tensor(name, shape, dt))

        def sem(name):
            return ctx.enter_context(nc.semaphore(name))

        def cols(b, nb):
            return slice(b * P, (b + nb) * P)

        half_shared = BLOCKS * COLS // 8
        table = nc.dram_tensor("table", [NODES, P], F32).ap()
        src_table = nc.dram_tensor("src_table", [NODES, 3 * P], BF16).ap()
        dst_table = nc.dram_tensor("dst_table", [3, COLS, P], BF16).ap()
        edge_table = nc.dram_tensor("edge_table", [3 * ED, QUARTERS * QCOLS], BF16).ap()
        dst_short = nc.dram_tensor("dst_short", [CHUNKS, CHUNK], I16).ap()

        bank = [ctx.enter_context(nc.psum_tensor(f"bank{i}", [P, CHUNK], F32)) for i in range(8)]

        wg = sb("wg", [P, LAYERS, P])
        wg_now = sb("wg_now", [P, P])
        bg = sb("bg", [P, LAYERS])
        bg_now = sb("bg_now", [P, 1])
        w1ab = sb("w1ab", [P, 2 * P])
        w1c = sb("w1c", [3 * ED, P])
        w1c_parts = sb("w1c_parts", [3 * ED, 3, P], BF16)
        w2 = sb("w2", [P, P])
        w3 = sb("w3", [P, P])
        u1a = sb("u1a", [P, P])
        u1b = sb("u1b", [P, P])
        u2 = sb("u2", [P, P])
        u3 = sb("u3", [P, P])
        b1_col = sb("b1_col", [P, 1])
        b3_col = sb("b3_col", [P, 1])
        c1_col = sb("c1_col", [P, 1])
        c2_col = sb("c2_col", [P, 1])
        c3_row = sb("c3_row", [P, P])
        g_row = sb("g_row", [P, P])
        be_row = sb("be_row", [P, P])
        b2_rep = sb("b2_rep", [3, P])
        b2_left = sb("b2_left", [3, 2, P])
        b2_part = sb("b2_part", [3, 3, P], BF16)
        b2_split = sb("b2_split", [3, TPC, P], BF16)
        ones_bf = sb("ones_bf", [3, P], BF16)
        ones = sb("ones", [P, P])
        ident = sb("ident", [P, P])
        eps_col = sb("eps_col", [P, 1])
        win_i = sb("win_i", [P, WIN], I32)
        win_iota = sb("win_iota", [P, WIN])
        part_i = sb("part_i", [P, 1], I32)
        part_iota = sb("part_iota", [P, 1])
        step_i = sb("step_i", [P, MAXPASS], I32)
        steps_f = sb("steps_f", [P, MAXPASS])
        key_iota = sb("key_iota", [P, KEYS], I16)
        node_iota = sb("node_iota", [P, P])
        ones_b = sb("ones_b", [P, P], BF16)
        ident_b = sb("ident_b", [P, P], BF16)

        src_sb = sb("src_sb", [P, TILES], I32)
        dst_sb = sb("dst_sb", [P, TILES], I32)
        dst_f = sb("dst_f", [P, TILES])
        dst_rows = sb("dst_rows", [CHUNKS, CHUNK], I32)
        lo_hi = sb("lo_hi", [CHUNKS, 2])
        diag = sb("diag", [CHUNKS, 2, CHUNKS])
        lo_all = sb("lo_all", [P, CHUNKS])
        span = sb("span", [P, CHUNKS])
        span_max = sb("span_max", [P, 1])
        over = sb("over", [P, MAXPASS])
        pass_f = sb("pass_f", [P, 1])
        pass_i = sb("pass_i", [P, 1], I32)
        pass_off = sb("pass_off", [P, 1])
        win_lo = sb("win_lo", [P, CHUNKS])
        win_lo_i = sb("win_lo_i", [P, CHUNKS], I32)
        win_word = sb("win_word", [P, CHUNKS], I32)
        win_shift = sb("win_shift", [P, CHUNKS])
        rel = sb("rel", [P, TILES])
        src_place = sb("src_place", [P, TILES])
        src_neg = sb("src_neg", [P, TILES])
        src_block = sb("src_block", [P, TILES])
        key = sb("key", [P, TILES])
        deg_max = sb("deg_max", [P, 1])
        sparse_i = sb("sparse_i", [P, 1], I32)
        win_node = sb("win_node", [3 * WIN, CHUNKS])
        part_node = sb("part_node", [P, 1])
        dst_rows_s = sb("dst_rows_s", [CHUNKS, CHUNK], I16)

        x_nm = sb("x_nm", [P, BLOCKS, P])
        h_nm = sb("h_nm", [P, BLOCKS, P])
        h_fm = sb("h_fm", [P, NODES])
        wide = sb("wide", [P, 3 * NODES // 2])
        agg = wide[:, 0:COLS]
        parts = wide[:, :].bitcast(BF16).rearrange("p (s n) -> p s n", s=3)
        deg = sb("deg", [P, COLS])
        dinv = sb("dinv", [P, NODES])
        shared = sb("shared", [P, BLOCKS * COLS // 4])
        counts = shared[:, :].bitcast(U8).rearrange("p (b c) -> p b c", c=COLS)
        used = 0

        def carve(shape, dt=F32):
            nonlocal used
            size = 4
            n = 1
            for d in shape[1:]:
                n *= d
            size = n * {F32: 4, I32: 4, BF16: 2, I16: 2}[dt] // 4
            part = shared[0:shape[0], used:used + size].bitcast(dt)
            used += size
            assert used <= BLOCKS * COLS // 4
            names = "abc"[:len(shape) - 1]
            dims = {c: d for c, d in zip(names[1:], shape[2:])}
            return part.rearrange(f"p ({' '.join(names)}) -> p {' '.join(names)}", **dims) if len(names) > 1 else part

        part_left = sb("part_left", [P, 2, CHUNK])
        counts_bf = h_nm[:, :, :].rearrange("p b f -> p (b f)").bitcast(BF16).rearrange("p (s n) -> p s n", s=2)
        key_onehot = wide[:, :].bitcast(BF16)[:, 0:2 * TPC * KEYS].rearrange(
            "p (s t k) -> p s t k", s=2, t=TPC)
        left = part_left[:, :, :].rearrange("p s n -> p (s n)")
        inside = left[:, 0:2 * TILES].rearrange("p (s t) -> p s t", s=2)
        key_i = wide[:, 0:KEYS].bitcast(I32)
        src_i = wide[:, KEYS:KEYS + TILES].bitcast(I32)
        low_bits = wide[:, 0:CHUNKS].bitcast(I32)
        squares = counts_bf[:, :, :].rearrange("p s n -> p (s n)").bitcast(F32)[:, 0:2 * TPC * P].rearrange(
            "p (s t r) -> p s t r", s=2, t=TPC)
        win_onehot = left[:, 0:TPC * WIN].bitcast(BF16).rearrange(
            "p (s t w) -> p s t w", s=2, t=TPC)
        src_onehot = left[:, TPC * WIN:TPC * (WIN + P)].bitcast(BF16).rearrange(
            "p (s t r) -> p s t r", s=2, t=TPC)
        sum_words = h_nm[:, BLOCKS - 5:BLOCKS, :].rearrange("p b f -> p (b f)").bitcast(I32)[:, 0:2 * KEYS // 4].rearrange(
            "p (s b w) -> p s b w", s=2, b=BLOCKS)
        sum_bytes = h_nm[:, BLOCKS - 5:BLOCKS, :].rearrange("p b f -> p (b f)").bitcast(U8)[:, 0:2 * KEYS].rearrange(
            "p (s k) -> p s k", s=2)
        count_words = shared[:, :].bitcast(I32).rearrange("p (b c) -> p b c", c=COLS // 4)
        dinv_nm = left[:, 0:BLOCKS]
        dinv_diag = h_nm
        stats = sb("stats", [P, BLOCKS, 6])
        mv = sb("mv", [P, BLOCKS, 2])
        rstd = sb("rstd", [P, BLOCKS])
        shift = sb("shift", [P, BLOCKS])

        idx = sb("idx", [P, SLOTS * TPC], I32)
        rows_b = carve([P, SLOTS * TPC, 3 * P], BF16)
        rows = rows_b[:, :, :].rearrange("p j f -> p (j f)")[:, 0:2 * SLOTS * TPC * P].bitcast(F32).rearrange(
            "p (j f) -> p j f", f=P)
        onehot = carve([P, SLOTS, TPC, WIN])
        onehot_t = carve([3 * WIN, SLOTS, CHUNK], BF16)
        dst_bc = carve([3 * WIN, SLOTS, CHUNK], I16)
        dst_win = carve([3 * WIN, SLOTS, P], BF16)
        edge_in = carve([3 * ED, SLOTS, CHUNK], BF16)
        r1 = carve([P, 2, CHUNK])
        r2 = carve([P, SLOTS, CHUNK])
        t1 = carve([P, 2, CHUNK])
        t2 = carve([P, 4, CHUNK])

        used = 0
        stage = carve([P, BLOCKS, P])
        used = 0
        src_stage = carve([P, BLOCKS, 3 * P], BF16).rearrange("p b (s f) -> p b s f", s=3)
        dst_stage = carve([P, 3 * BLOCKS, P], BF16).rearrange("p (s b) f -> p s b f", s=3)
        left_over = carve([P, 4, CHUNK])
        XB = 5 * SPLIT // 2 // P
        x_flat = x_nm[:, 0:XB, :].rearrange("p b f -> p (b f)")
        feat = x_flat[:, 0:SPLIT]
        feat_parts = x_flat[:, SPLIT:5 * SPLIT // 2].bitcast(BF16).rearrange("p (s n) -> p s n", s=3)
        assert XB <= FULL

        loaded = sem("loaded")
        first_sem = loaded.num
        loaded_idx = sem("loaded_idx")
        loaded_x = sem("loaded_x")
        pool_done = sem("pool_done")
        dve_done = sem("dve_done")
        act_done = sem("act_done")
        pe_done = sem("pe_done")
        pe2_done = sem("pe2_done")
        pe3_done = sem("pe3_done")
        stored = sem("stored")
        idx_ready = sem("idx_ready")
        onehot_ready = sem("onehot_ready")
        onehot_t_ready = sem("onehot_t_ready")
        seg_done = sem("seg_done")
        window_added = sem("window_added")
        z_done = sem("z_done")
        gathers_begun = sem("gathers_begun")
        relu1_done = sem("relu1_done")
        y_done = sem("y_done")
        relu2_done = sem("relu2_done")
        dst_bc_in = [sem(f"dst_bc_in{k}") for k in range(SLOTS)]
        dst_win_in = [sem(f"dst_win_in{k}") for k in range(SLOTS)]
        edge_in_in = [sem(f"edge_in_in{k}") for k in range(SLOTS)]
        keys_ready = sem("keys_ready")
        counted = sem("counted")
        degrees_added = sem("degrees_added")
        sums_copied = sem("sums_copied")
        squared = sem("squared")
        sums3_done = sem("sums3_done")
        third_done = sem("third_done")
        hidden1_done = sem("hidden1_done")
        hidden2_done = sem("hidden2_done")
        updated = sem("updated")
        rooted = sem("rooted")
        gained = sem("gained")
        feat_in = sem("feat_in")
        feat_split = sem("feat_split")
        split_begun = sem("split_begun")
        feat_stored = sem("feat_stored")
        block_ready = [sem(f"block_ready{n}") for n in range(2)]
        block_used = sem("block_used")
        gathered = [sem(f"gathered{j}") for j in range(SLOTS * TPC)]
        all_sems = [loaded, loaded_idx, loaded_x, pool_done, dve_done, act_done, pe_done, pe2_done, pe3_done, stored,
                    idx_ready, onehot_ready, onehot_t_ready, seg_done, window_added, gathers_begun, z_done, relu1_done, y_done,
                    relu2_done, keys_ready, counted, degrees_added, sums_copied, squared, sums3_done, third_done, hidden1_done, hidden2_done, updated, rooted, gained, feat_in, feat_split, split_begun, feat_stored, *block_ready, block_used, *dst_bc_in, *dst_win_in, *edge_in_in, *gathered]
        nums = sorted(s.num for s in all_sems)
        assert nums == list(range(nums[0], nums[-1] + 1))
        gathers = sorted(s.num for s in gathered)

        @contextmanager
        def phase(name, gather=False):
            with nc.Block(name) as block:
                yield block
            if gather:
                nc.gpsimd.dma_reset(range(gathers[0], gathers[-1] + 1))
            nc.all_engine_barrier(sems_to_clear=range(nums[0], nums[-1] + 1))

        class Chain:

            def __init__(self, eng, s):
                self.eng, self.s, self.n = eng, s, 0

            def __call__(self, ins):
                self.n += 1
                ins.then_inc(self.s, 1)
                self.eng.wait_ge(self.s, self.n)

        def norm_dve(dve, link, frm):
            for b in range(BLOCKS):
                ins = dve.bn_stats(stats[:, b, :], frm[:, b, :])
            link(ins)
            for b in range(BLOCKS):
                ins = dve.bn_aggr(mv[:, b, :], stats[:, b, :])
            ins.then_inc(z_done, 1)
            dve.wait_ge(y_done, 1)
            link(dve.reciprocal(rstd[:, :], rstd[:, :]))
            dve.scalar_tensor_tensor(out=shift[:, :], in0=mv[:, :, 0], scalar=-1.0, in1=rstd[:, :],
                                     op0=ALU.mult, op1=ALU.mult).then_inc(relu1_done, 1)

        def norm_act(act, frm, to, func):
            act.wait_ge(z_done, 1)
            act.activation(rstd[:, :], mv[:, :, 1], ACT.Sqrt, bias=eps_col[:, 0:1]).then_inc(y_done, 1)
            act.wait_ge(relu1_done, 1)
            for b, nb in GROUPS:
                for t in range(b, b + nb):
                    ins = act.activation(to[:, t, :], frm[:, t, :], func, bias=shift[:, t:t + 1], scale=rstd[:, t:t + 1])
                ins.then_inc(relu2_done, 1)

        def to_feature_major(pe):
            for n, (b, nb) in enumerate(GROUPS):
                pe.wait_ge(relu2_done, n + 1)
                for t in range(nb):
                    last = pe.transpose(bank[n][:, t * P:(t + 1) * P], h_nm[:, b + t, :], ident[:, :])
                last.then_inc(pe2_done, 1)

        with phase("load") as block:
            @block.sync
            def _(sp):
                sp.dma_start(dst_rows[:, :], dst_flat.rearrange("(c e) -> c e", e=CHUNK)).then_inc(loaded_idx, 16)
                sp.dma_start(dst_sb[:, :], dst_pt).then_inc(loaded_idx, 16)
                sp.dma_start(src_sb[:, :], src_pt).then_inc(loaded_idx, 16)
                sp.wait_ge(pool_done, 1)
                sp.dma_start(x_nm[:, 0:FULL, :], x[0:FULL * P, :].rearrange("(b p) f -> p b f", p=P)).then_inc(loaded_x, 16)
                sp.dma_start(x_nm[0:REST, FULL, :], x[FULL * P:N, :]).then_inc(loaded_x, 16)
                sp.wait_ge(loaded_x, 32)
                sp.wait_ge(pool_done, 11)
                for part in range(3):
                    sp.dma_start(dst_table[part, NODES:COLS, :], ones_b[0:COLS - NODES, :]).then_inc(stored, 16)
                sp.wait_ge(keys_ready, 1)
                sp.dma_start(dst_short, dst_rows_s[:, :]).then_inc(stored, 16)
                sp.wait_ge(stored, 64)

            @block.scalar
            def _(act):
                def col(v):
                    return v.rearrange("(p o) -> p o", o=1)

                def row(v, n):
                    return v.rearrange("(o f) -> o f", o=1).to_broadcast([n, P])

                small = [(wg[:, l, :], w_gcn[l]) for l in range(LAYERS)]
                small += [(bg[:, l:l + 1], col(b_gcn[l])) for l in range(LAYERS)]
                small += [(w1ab[:, 0:P], msg_w[0][0:P, :]), (w1ab[:, P:2 * P], msg_w[0][P:2 * P, :]),
                          *((w1c[r * ED:(r + 1) * ED, :], msg_w[0][2 * P:2 * P + ED, :]) for r in range(3)), (w2[:, :], msg_w[1]), (w3[:, :], msg_w[2]),
                          (u1a[:, :], upd_w[0][0:P, :]), (u1b[:, :], upd_w[0][P:2 * P, :]), (u2[:, :], upd_w[1]),
                          (u3[:, :], upd_w[2]), (b1_col[:, :], col(msg_b[0])), (b2_rep[:, :], row(msg_b[1], 3)),
                          (b3_col[:, :], col(msg_b[2])), (c1_col[:, :], col(upd_b[0])), (c2_col[:, :], col(upd_b[1])),
                          (c3_row[:, :], row(upd_b[2], P)), (g_row[:, :], row(ln_g, P)), (be_row[:, :], row(ln_b, P))]
                for to, frm in small:
                    act.dma_start(to, frm).then_inc(loaded, 16)
                act.wait_ge(loaded, 16 * len(small))
                act.sem_inc(act_done, 1)
                norm_act(act, x_nm, h_nm, ACT.Relu)

            @block.gpsimd
            def _(pool):
                pool.memset(x_nm[:, FULL:BLOCKS, :], 0.0).then_inc(pool_done, 1)
                pool.memset(ones[:, :], 1.0).then_inc(pool_done, 1)
                pool.memset(ident[:, :], 0.0).then_inc(pool_done, 1)
                pool.wait_ge(pool_done, 3)
                pool.affine_select(out=ident[:, :], in_=ident[:, :], compare_op=ALU.not_equal, fill=1.0,
                                   base=0, pattern=[[-1, P]], channel_multiplier=1).then_inc(pool_done, 1)
                pool.iota(win_i[:, :], pattern=[[1, WIN]], base=0, channel_multiplier=0).then_inc(pool_done, 1)
                pool.iota(part_i[:, :], pattern=[[0, 1]], base=0, channel_multiplier=1).then_inc(pool_done, 1)
                pool.iota(step_i[:, :], pattern=[[WIN, MAXPASS]], base=0, channel_multiplier=0).then_inc(pool_done, 1)
                pool.iota(key_i[:, :], pattern=[[1, KEYS]], base=0, channel_multiplier=0).then_inc(pool_done, 1)
                pool.memset(eps_col[:, :], EPS).then_inc(pool_done, 1)
                pool.memset(ones_bf[:, :], 1.0)
                pool.memset(shared[:, 0:half_shared], 0.0).then_inc(pool_done, 1)
                pool.memset(ones_b[:, :], 1.0).then_inc(pool_done, 1)
                pool.memset(deg[:, :], 0.0)

            @block.vector
            def _(dve):
                link = Chain(dve, dve_done)
                dve.wait_ge(loaded_idx, 48)
                dve.tensor_copy(dst_f[:, :], dst_sb[:, :])
                dve.tensor_copy(dst_rows_s[:, :], dst_rows[:, :]).then_inc(keys_ready, 1)
                dve.tensor_reduce(lo_hi[:, 0:1], dst_rows[:, :], AX.X, ALU.min)
                link(dve.tensor_reduce(lo_hi[:, 1:2], dst_rows[:, :], AX.X, ALU.max))
                dve.wait_ge(pool_done, 9)
                dve.tensor_scalar(diag[:, 0, :], ident[0:CHUNKS, 0:CHUNKS], lo_hi[:, 0:1], None, ALU.mult)
                dve.tensor_scalar(diag[:, 1, :], ident[0:CHUNKS, 0:CHUNKS], lo_hi[:, 1:2], None, ALU.mult).then_inc(onehot_ready, 1)
                dve.tensor_copy(win_iota[:, :], win_i[:, :])
                dve.tensor_copy(ident_b[:, :], ident[:, :])
                dve.tensor_copy(part_iota[:, :], part_i[:, :])
                dve.tensor_copy(key_iota[:, 0:KEYS], key_i[:, :])
                dve.tensor_copy(node_iota[:, :], key_i[:, 0:P])
                link(dve.tensor_scalar(src_i[:, :], src_sb[:, :], P - 1, None, ALU.bitwise_and))
                dve.tensor_copy(src_place[:, :], src_i[:, :])
                link(dve.tensor_scalar(src_neg[:, :], src_i[:, :], -1.0, None, ALU.mult))
                link(dve.tensor_scalar(src_i[:, :], src_sb[:, :], P.bit_length() - 1, None, ALU.logical_shift_right))
                dve.tensor_copy(src_block[:, :], src_i[:, :])
                link(dve.tensor_copy(steps_f[:, :], step_i[:, :]))
                dve.wait_ge(pe_done, 1)
                link(dve.tensor_copy(lo_all[:, :], bank[7][:, 0:CHUNKS]))
                link(dve.tensor_tensor(span[:, :], bank[7][:, CHUNKS:2 * CHUNKS], lo_all[:, :], ALU.subtract))
                link(dve.tensor_reduce(span_max[:, :], span[:, :], AX.X, ALU.max))
                link(dve.tensor_scalar(over[:, :], steps_f[:, :], span_max[:, 0:1], None, ALU.is_le))
                link(dve.tensor_reduce(pass_f[:, :], over[:, :], AX.X, ALU.add))
                link(dve.tensor_copy(pass_i[:, :], pass_f[:, :]))
                link(dve.tensor_scalar(part_node[:, :], part_iota[:, :], float(WIN), -float(WIN), ALU.is_ge, ALU.mult))
                link(dve.tensor_tensor(part_node[:, :], part_node[:, :], part_iota[:, :], ALU.add))
                link(dve.tensor_scalar(span_max[:, :], part_iota[:, :], 2.0 * WIN, -float(WIN), ALU.is_ge, ALU.mult))
                link(dve.tensor_tensor(part_node[:, :], part_node[:, :], span_max[:, :], ALU.add))
                dve.wait_ge(act_done, 1)
                for part in range(3):
                    link(dve.tensor_copy(w1c_parts[:, part, :], w1c[:, :]))
                    if part < 2:
                        link(dve.tensor_tensor(w1c[:, :], w1c[:, :], w1c_parts[:, part, :], ALU.subtract))
                dve.wait_ge(act_done, 1)
                link(dve.tensor_copy(b2_part[:, 0, :], b2_rep[:, :]))
                link(dve.tensor_tensor(b2_left[:, 0, :], b2_rep[:, :], b2_part[:, 0, :], ALU.subtract))
                link(dve.tensor_copy(b2_part[:, 1, :], b2_left[:, 0, :]))
                link(dve.tensor_tensor(b2_left[:, 1, :], b2_left[:, 0, :], b2_part[:, 1, :], ALU.subtract))
                link(dve.tensor_copy(b2_part[:, 2, :], b2_left[:, 1, :]))
                for s in range(3):
                    link(dve.tensor_scalar(b2_left[:, s % 2, :], b2_part[:, s, :], ident[0:3, s:s + 1], None, ALU.mult)
                         if s == 0 else
                         dve.scalar_tensor_tensor(out=b2_left[:, s % 2, :], in0=b2_part[:, s, :], scalar=ident[0:3, s:s + 1],
                                                  in1=b2_left[:, (s + 1) % 2, :], op0=ALU.mult, op1=ALU.add))
                for t in range(TPC):
                    dve.tensor_copy(b2_split[:, t, :], b2_left[:, 0, :])
                dve.wait_ge(loaded_x, 32)
                norm_dve(dve, link, x_nm)
                link(dve.memset(shared[:, half_shared:], 0.0))
                dve.wait_ge(pool_done, 10)
                for b in range(BLOCKS):
                    dve.tensor_copy(counts[:, b, cols(b, 1)], ident[:, :])
                for n, (b, nb) in enumerate(GROUPS):
                    dve.wait_ge(pe2_done, n + 1)
                    dve.tensor_copy(h_fm[:, cols(b, nb)], bank[n][:, 0:nb * P])

            @block.tensor
            def _(pe):
                pe.wait_ge(onehot_ready, 1)
                pe.matmul(bank[7][:, 0:2 * CHUNKS], ones[0:CHUNKS, :], diag[:, :, :].rearrange("p a c -> p (a c)"),
                          start=True, stop=True).then_inc(pe_done, 1)
                to_feature_major(pe)

        passes = nc.values_load(pass_i[0:1, 0:1], min_val=1, max_val=MAXPASS)

        def edge_passes(name, engines, gather=False):
            with phase(f"{name}_start") as block:
                @block.vector
                def _(dve):
                    dve.memset(pass_off[:, :], 0.0)

            with nc.Fori(0, passes):
                with phase(f"{name}_windows") as block:
                    @block.vector
                    def _(dve):
                        link = Chain(dve, dve_done)
                        link(dve.tensor_scalar(win_lo[:, :], lo_all[:, :], pass_off[:, 0:1], float(NODES), ALU.add, ALU.min))
                        link(dve.tensor_copy(win_lo_i[:, :], win_lo[:, :]))
                        dve.tensor_scalar(win_node[:, :], win_lo[0:3 * WIN, :], part_node[0:3 * WIN, 0:1], None, ALU.add)
                        dve.tensor_tensor(rel[:, :].rearrange("p (c t) -> p c t", t=TPC),
                                          dst_f[:, :].rearrange("p (c t) -> p c t", t=TPC),
                                          win_lo[:, :].unsqueeze(2).to_broadcast([P, CHUNKS, TPC]), ALU.subtract)
                        link(dve.tensor_scalar(pass_off[:, :], pass_off[:, :], float(WIN), None, ALU.add))
                        if name == "count":
                            count_windows(dve, link)

                with phase(f"{name}_edges", gather=gather) as block:
                    engines(block)

        def edge_engines(block, target, rows_of, messages):
            z = [bank[0], bank[1]]
            y = [bank[2], bank[3]]
            acc = [bank[4], bank[5]]

            @block.vector
            def _(dve):
                def indices(i, k):
                    if rows_of is not None:
                        dve.wait_ge(z_done if messages else seg_done, i * SLOTS + k + 1)
                        dve.tensor_copy(idx[:, k * TPC:(k + 1) * TPC],
                                        src_sb[:, bass.ds((i * SLOTS + k) * TPC, TPC)]).then_inc(idx_ready, 1)

                def prepare(i, k):
                    dve.wait_ge(seg_done, i * SLOTS + k + 1)
                    dve.tensor_tensor(
                        onehot[:, k, :, :],
                        rel[:, bass.ds((i * SLOTS + k) * TPC, TPC)].unsqueeze(2).to_broadcast([P, TPC, WIN]),
                        win_iota[:, :].unsqueeze(1).to_broadcast([P, TPC, WIN]),
                        ALU.is_equal).then_inc(onehot_ready, 1)
                    if messages:
                        dve.wait_ge(dst_bc_in[k], 16 * (i + 1))
                        dve.tensor_scalar(onehot_t[:, k, :], dst_bc[:, k, :], win_node[:, bass.ds(i * SLOTS + k, 1)],
                                          None, ALU.is_equal).then_inc(onehot_t_ready, 1)

                def add_window(i, k):
                    at = dve.value_load(win_lo_i[0:1, bass.ds(i * SLOTS + k, 1)], min_val=0, max_val=NODES)
                    dve.wait_ge(seg_done, i * SLOTS + k + 1 + SLOTS)
                    dve.wait_ge(window_added, i * SLOTS + k + 2)
                    w = target[:, bass.ds(at, WIN)]
                    dve.tensor_tensor(w, w, acc[k % 2][:, 0:WIN], ALU.add).then_inc(window_added, 1)

                for k in range(SLOTS):
                    indices(0, k)
                    prepare(0, k)
                lag = 2 if messages else 0
                with dve.Fori(0, ITERS - 1) as i:
                    for k in range(SLOTS + lag):
                        if k >= lag:
                            add_window(i, k - lag)
                        if k < SLOTS:
                            indices(i + 1, k)
                        if k >= lag:
                            prepare(i + 1, k - lag)
                for k in range(SLOTS):
                    add_window(ITERS - 1, k)

            @block.gpsimd
            def _(pool):
                if rows_of is None:
                    return
                with pool.Fori(0, ITERS) as i:
                    for k in range(SLOTS):
                        pool.wait_ge(idx_ready, i * SLOTS + k + 1)
                        pool.sem_inc(gathers_begun, 1)
                        for j in range(k * TPC, (k + 1) * TPC):
                            pool.indirect_dma_start(
                                out=(rows_b if messages else rows)[:, j, :], out_offset=None, in_=rows_of,
                                in_offset=bass.IndirectOffsetOnAxis(ap=idx[:, j:j + 1].bitcast(U32), axis=0),
                            ).then_inc(gathered[j], 16)

            @block.sync
            def _(sp):
                if not messages:
                    return
                with sp.Fori(0, ITERS) as i:
                    for k in range(SLOTS):
                        c = i * SLOTS + k
                        at = sp.value_load(win_lo_i[0:1, bass.ds(c, 1)], min_val=0, max_val=NODES)
                        sp.wait_ge(z_done, c + 1)
                        sp.dma_start(dst_bc[:, k, :], dst_short[bass.ds(c, 1), :].to_broadcast([3 * WIN, CHUNK])
                                     ).then_inc(dst_bc_in[k], 16)
                        sp.dma_start(edge_in[:, k, :], edge_table[:, bass.ds(c * CHUNK, CHUNK)]).then_inc(edge_in_in[k], 16)
                        for part in range(3):
                            sp.dma_start(dst_win[part * WIN:(part + 1) * WIN, k, :],
                                         dst_table[part, bass.ds(at, WIN), :]).then_inc(dst_win_in[k], 16)

            @block.scalar
            def _(act):
                if not messages:
                    return

                def relu1(i, k):
                    act.wait_ge(z_done, i * SLOTS + k + 1 + SLOTS)
                    act.wait_ge(y_done, i * SLOTS + k + 1)
                    act.activation(r1[:, k % 2, :], z[k % 2][:, :], ACT.Relu, bias=b1_col[:, 0:1]).then_inc(relu1_done, 1)

                def relu2(i, k):
                    act.wait_ge(y_done, i * SLOTS + k + 1 + 2)
                    act.wait_ge(seg_done, i * SLOTS + k + 1)
                    act.activation(r2[:, k, :], y[k % 2][:, :], ACT.Relu).then_inc(relu2_done, 1)

                with act.Fori(0, ITERS) as i:
                    for k in range(SLOTS + 1):
                        if k < SLOTS:
                            relu1(i, k)
                        if k >= 1:
                            relu2(i, k - 1)

            @block.tensor
            def _(pe):
                pe.sem_inc(seg_done, SLOTS)
                pe.sem_inc(window_added, 2)
                if messages:
                    pe.sem_inc(z_done, SLOTS)
                    pe.sem_inc(relu1_done, 2)
                    pe.sem_inc(y_done, 2)
                    pe.sem_inc(relu2_done, 2)

                def first(i, k):
                    c = i * SLOTS + k
                    pe.wait_ge(relu1_done, c + 1)
                    pe.wait_ge(edge_in_in[k], 16 * (i + 1))
                    for part in range(3):
                        n = (3 - part) * ED
                        pe.matmul(z[k % 2][:, :], w1c_parts[0:n, part, :], edge_in[0:n, k, :], start=(part == 0), stop=False)
                    pe.wait_ge(dst_win_in[k], 48 * (i + 1))
                    pe.wait_ge(onehot_t_ready, c + 1)
                    pe.matmul(z[k % 2][:, :], dst_win[:, k, :], onehot_t[:, k, :], start=False, stop=False)
                    for t in range(TPC):
                        pe.wait_ge(gathered[k * TPC + t], 16 * (i + 1))
                        for part in range(3):
                            last = pe.matmul(z[k % 2][:, t * P:(t + 1) * P],
                                             rows_b[:, k * TPC + t, part * P:(part + 1) * P], ident_b[:, :],
                                             start=False, stop=(t == TPC - 1 and part == 2))
                    last.then_inc(z_done, 1)

                def second(i, k):
                    c = i * SLOTS + k
                    pe.wait_ge(relu2_done, c + 1)
                    pe.matmul(y[k % 2][:, :], ones_bf[:, :], b2_split[:, :, :].rearrange("p t f -> p (t f)"),
                              start=True, stop=False)
                    pe.wait_ge(relu1_done, c + 1 + 2)
                    for t in range(TPC):
                        last = pe.matmul(y[k % 2][:, t * P:(t + 1) * P], r1[:, k % 2, t * P:(t + 1) * P], w2[:, :],
                                         start=False, stop=(t == TPC - 1))
                    last.then_inc(y_done, 1)

                def summed(i, k):
                    c = i * SLOTS + k
                    pe.wait_ge(onehot_ready, c + 1)
                    pe.wait_ge(window_added, c + 1)
                    if messages:
                        pe.wait_ge(relu2_done, c + 1 + 2)
                    for t in range(TPC):
                        if messages:
                            what = r2[:, k, t * P:(t + 1) * P]
                        elif rows_of is not None:
                            pe.wait_ge(gathered[k * TPC + t], 16 * (i + 1))
                            what = rows[:, k * TPC + t, :]
                        else:
                            what = ones[:, :]
                        last = pe.matmul(acc[k % 2][:, 0:WIN], what, onehot[:, k, t, :],
                                         start=(t == 0), stop=(t == TPC - 1))
                    last.then_inc(seg_done, 1)

                with pe.Fori(0, ITERS) as i:
                    for k in range(SLOTS + 2):
                        if messages and k < SLOTS:
                            first(i, k)
                        if messages and 1 <= k <= SLOTS:
                            second(i, k - 1)
                        if k >= 2:
                            summed(i, k - 2)

        def count_windows(dve, link):
            dve.tensor_scalar(win_word[:, :], win_lo_i[:, :], 2, None, ALU.logical_shift_right)
            link(dve.tensor_scalar(low_bits[:, :], win_lo_i[:, :], 3, None, ALU.bitwise_and))
            dve.tensor_copy(win_shift[:, :], low_bits[:, :])
            dve.tensor_scalar(inside[:, 0, :], rel[:, :], 0.0, None, ALU.is_ge)
            link(dve.scalar_tensor_tensor(out=key[:, :], in0=src_block[:, :], scalar=float(CWIN), in1=rel[:, :],
                                          op0=ALU.mult, op1=ALU.add))
            key_ct = key[:, :].rearrange("p (c t) -> p c t", t=TPC)
            link(dve.tensor_tensor(key_ct, key_ct, win_shift[:, :].unsqueeze(2).to_broadcast([P, CHUNKS, TPC]), ALU.add))
            link(dve.tensor_scalar(inside[:, 1, :], rel[:, :], float(WIN), None, ALU.is_lt))
            link(dve.tensor_tensor(inside[:, 0, :], inside[:, 0, :], inside[:, 1, :], ALU.mult))
            link(dve.scalar_tensor_tensor(out=key[:, :], in0=key[:, :], scalar=1.0, in1=inside[:, 0, :],
                                          op0=ALU.add, op1=ALU.mult))
            dve.tensor_scalar(key[:, :], key[:, :], -1.0, None, ALU.add)

        def count_engines(block):
            sums = [[bank[0], bank[1], bank[2]], [bank[3], bank[4], bank[5]]]
            degs = [bank[6], bank[7]]

            @block.vector
            def _(dve):
                def prepare(i, k):
                    c = i * SLOTS + k
                    dve.wait_ge(counted, c + 1)
                    for t in range(TPC):
                        at = bass.ds(c * TPC + t, 1)
                        dve.tensor_scalar(key_onehot[:, k % 2, t, 0:KEYS], key_iota[:, 0:KEYS], key[:, at], None, ALU.is_equal)
                        if t < TPC // 2:
                            dve.tensor_scalar(src_onehot[:, k % 2, t, :], key_iota[:, 0:P], src_place[:, at], None, ALU.is_equal)
                    dve.tensor_tensor(
                        win_onehot[:, k % 2, :, :],
                        rel[:, bass.ds(c * TPC, TPC)].unsqueeze(2).to_broadcast([P, TPC, WIN]),
                        win_iota[:, :].unsqueeze(1).to_broadcast([P, TPC, WIN]),
                        ALU.is_equal).then_inc(keys_ready, 1)

                def add_degrees(i, k):
                    c = i * SLOTS + k
                    at = dve.value_load(win_lo_i[0:1, bass.ds(c, 1)], min_val=0, max_val=NODES)
                    dve.wait_ge(counted, c + 1 + 2)
                    dve.wait_ge(degrees_added, c + 2)
                    w = deg[:, bass.ds(at, WIN)]
                    dve.tensor_tensor(w, w, degs[k % 2][:, 0:WIN], ALU.add).then_inc(degrees_added, 1)

                prepare(0, 0)
                with dve.Fori(0, ITERS - 1) as i:
                    for k in range(SLOTS):
                        prepare(i + (k + 1) // SLOTS, (k + 1) % SLOTS)
                        add_degrees(i, k)
                for k in range(SLOTS):
                    if k + 1 < SLOTS:
                        prepare(ITERS - 1, k + 1)
                    add_degrees(ITERS - 1, k)

            @block.tensor
            def _(pe):
                pe.sem_inc(counted, 2)
                pe.sem_inc(degrees_added, 2)
                pe.sem_inc(sums_copied, 2)
                pe.sem_inc(window_added, 2)
                with pe.Fori(0, ITERS) as i:
                    for k in range(SLOTS):
                        c = i * SLOTS + k
                        pe.wait_ge(keys_ready, c + 1)
                        pe.wait_ge(degrees_added, c + 1)
                        pe.wait_ge(sums_copied, c + 1)
                        for t in range(TPC):
                            pe.matmul(degs[k % 2][:, 0:WIN], ones_b[:, :], win_onehot[:, k % 2, t, :],
                                      start=(t == 0), stop=(t == TPC - 1))
                        pe.wait_ge(onehot_ready, c + 1)
                        for h, (b, nb) in enumerate(THIRDS):
                            for t in range(TPC):
                                last = pe.matmul(sums[k % 2][h][:, 0:nb * CWIN], src_onehot[:, k % 2, t, :],
                                                 key_onehot[:, k % 2, t, b * CWIN:(b + nb) * CWIN],
                                                 start=(t == 0), stop=(t == TPC - 1))
                        last.then_inc(counted, 1)

            @block.scalar
            def _(act):
                def sources(c, k):
                    act.wait_ge(counted, c + 1)
                    for t in range(TPC // 2, TPC):
                        ins = act.activation(squares[:, k % 2, t, :], node_iota[:, :], ACT.Square,
                                             bias=src_neg[:, bass.ds(c * TPC + t, 1)])
                    ins.then_inc(squared, 1)
                    act.wait_ge(squared, c + 1)
                    act.activation(src_onehot[:, k % 2, TPC // 2:, :], squares[:, k % 2, TPC // 2:, :], ACT.Relu,
                                   bias=1.0, scale=-1.0).then_inc(onehot_ready, 1)

                def copy_sums(c, k):
                    act.wait_ge(counted, c + 1 + 2)
                    act.wait_ge(window_added, c + 1)
                    for h, (b, nb) in enumerate(THIRDS):
                        ins = act.activation(sum_bytes[:, k % 2, b * CWIN:(b + nb) * CWIN], sums[k % 2][h][:, 0:nb * CWIN],
                                             ACT.Copy)
                    ins.then_inc(sums_copied, 1)

                sources(0, 0)
                with act.Fori(0, ITERS - 1) as i:
                    for k in range(SLOTS):
                        sources(i * SLOTS + k + 1, (k + 1) % SLOTS)
                        copy_sums(i * SLOTS + k, k)
                for k in range(SLOTS):
                    if k + 1 < SLOTS:
                        sources((ITERS - 1) * SLOTS + k + 1, k + 1)
                    copy_sums((ITERS - 1) * SLOTS + k, k)

            @block.gpsimd
            def _(pool):
                with pool.Fori(0, ITERS) as i:
                    for k in range(SLOTS):
                        c = i * SLOTS + k
                        at = pool.value_load(win_word[0:1, bass.ds(c, 1)], min_val=0, max_val=NODES // 4)
                        pool.wait_ge(sums_copied, c + 1 + 2)
                        pool.wait_ge(window_added, c + 2)
                        w = count_words[:, :, bass.ds(at, CWIN // 4)]
                        pool.tensor_tensor(w, w, sum_words[:, k % 2, :, :], ALU.add).then_inc(window_added, 1)

        edge_passes("count", count_engines)

        SPLIT_DMAS = QUARTERS * 16

        def split_on_pool(pool):
            with pool.Fori(0, LAYER_STEP + 1) as i:
                pool.wait_ge(feat_in, 16 * (i + 1))
                pool.sem_inc(split_begun, 1)
                pool.tensor_copy(feat_parts[:, 0, :], feat).then_inc(feat_split, 1)
                pool.wait_ge(feat_split, i * 4 + 1)
                pool.tensor_tensor(feat, feat, feat_parts[:, 0, :], ALU.subtract).then_inc(feat_split, 1)
                pool.wait_ge(feat_split, i * 4 + 2)
                pool.sem_inc(split_begun, 1)
                pool.tensor_copy(feat_parts[:, 1, :], feat).then_inc(feat_split, 1)
                pool.wait_ge(feat_split, i * 4 + 3)
                pool.tensor_tensor(feat_parts[:, 2, :], feat, feat_parts[:, 1, :], ALU.subtract).then_inc(feat_split, 1)

        def split_on_sync(sp, layer):
            sp.sem_inc(feat_stored, 3 * SPLIT_DMAS)
            with sp.Fori(0, LAYER_STEP + 1) as i:
                r = layer * LAYER_STEP + i
                sp.wait_ge(feat_stored, 3 * SPLIT_DMAS * (i + 1))
                sp.sem_inc(split_begun, 1)
                sp.dma_start(feat, edge_q[:, bass.ds(r * SPLIT, SPLIT)]).then_inc(feat_in, 16)
                for part, ready in enumerate((1, 3, 4)):
                    sp.wait_ge(feat_split, i * 4 + ready)
                    sp.sem_inc(split_begun, 1)
                    for q in range(QUARTERS):
                        sp.dma_start(edge_table[part * ED:(part + 1) * ED, bass.ds(r * SPLIT + q * QCOLS, SPLIT)],
                                     feat_parts[q * ED:(q + 1) * ED, part, :]).then_inc(feat_stored, 16)
            sp.wait_ge(feat_stored, 3 * SPLIT_DMAS * (LAYER_STEP + 2))

        def convert(eng, b, act):
            eng.wait_ge(block_used, b + 1)
            to, frm = counts_bf[:, b % 2, :], counts[:, b, 0:NODES]
            ins = eng.activation(to, frm, ACT.Copy) if act else eng.tensor_copy(to, frm)
            ins.then_inc(block_ready[b % 2], 1)

        with phase("degree") as block:
            @block.tensor
            def _(pe):
                for b in range(BLOCKS):
                    last = pe.matmul(bank[7][:, b:b + 1], deg[0:1, cols(b, 1)], ones[0:1, 0:1], start=True, stop=True)
                last.then_inc(pe_done, 1)
                for n, (b, nb) in enumerate(GROUPS):
                    pe.wait_ge(keys_ready, n + 1)
                    for t in range(nb):
                        last = pe.matmul(bank[n][:, t * P:(t + 1) * P], ones[:, :], dinv_diag[:, b + t, :],
                                         start=True, stop=True)
                    last.then_inc(pe2_done, 1)

            @block.scalar
            def _(act):
                act.wait_ge(pe_done, 1)
                act.activation(dinv_nm[:, :], bank[7][:, 0:BLOCKS], ACT.Sqrt, bias=1.0).then_inc(act_done, 1)
                for n, (b, nb) in enumerate(GROUPS):
                    act.wait_ge(pe2_done, n + 1)
                    act.activation(dinv[:, cols(b, nb)], bank[n][:, 0:nb * P], ACT.Copy).then_inc(relu1_done, 1)

            @block.vector
            def _(dve):
                link = Chain(dve, dve_done)
                link(dve.tensor_reduce(deg_max[:, :], deg[:, 0:N], AX.X, ALU.max))
                dve.tensor_scalar(sparse_i[:, :], deg_max[:, :], float(DENSE_MAX), None, ALU.is_gt)
                dve.wait_ge(act_done, 1)
                link(dve.reciprocal(dinv_nm[:, :], dinv_nm[:, :]))
                for b, nb in GROUPS:
                    for t in range(b, b + nb):
                        ins = dve.tensor_scalar(dinv_diag[:, t, :], ident[:, :], dinv_nm[:, t:t + 1], None, ALU.mult)
                    ins.then_inc(keys_ready, 1)
                for n, (b, nb) in enumerate(GROUPS):
                    dve.wait_ge(relu1_done, n + 1)
                    dve.tensor_tensor(h_fm[:, cols(b, nb)], h_fm[:, cols(b, nb)], dinv[:, cols(b, nb)], ALU.mult)

        sparse = nc.values_load(sparse_i[0:1, 0:1], min_val=0, max_val=1)

        with nc.Fori(0, LAYERS) as layer:
          with nc.If(sparse < 1):
            with phase("gcn_dense") as block:
                @block.tensor
                def _(pe):
                    def rows_out(n):
                        b, nb = GROUPS[n]
                        if n >= 1:
                            pe.wait_ge(y_done, n)
                        for t in range(nb):
                            last = pe.matmul(bank[7][:, t * P:(t + 1) * P], h_fm[:, cols(b + t, 1)], wg_now[:, :],
                                             start=True, stop=True)
                        last.then_inc(pe_done, 1)

                    def sums_of(n):
                        b, nb = GROUPS[n]
                        pe.wait_ge(relu2_done, n + 1)
                        for s in range(b, b + nb):
                            pe.wait_ge(block_ready[s % 2], s // 2 + 1)
                            for part in range(3):
                                for m, (g, ng) in enumerate(GROUPS):
                                    last = pe.matmul(bank[m][:, 0:ng * P], parts[:, part, cols(s, 1)],
                                                     counts_bf[:, s % 2, cols(g, ng)],
                                                     start=(s == 0 and part == 0), stop=(s == BLOCKS - 1 and part == 2))
                            last.then_inc(block_used, 1)

                    pe.sem_inc(block_used, 2)
                    pe.wait_ge(act_done, 1)
                    rows_out(0)
                    for n in range(NG):
                        if n + 1 < NG:
                            rows_out(n + 1)
                        sums_of(n)

                @block.gpsimd
                def _(pool):
                    split_on_pool(pool)

                @block.sync
                def _(sp):
                    split_on_sync(sp, layer)

                @block.scalar
                def _(act):
                    act.activation(wg_now[:, :], wg[:, bass.ds(layer, 1), :].rearrange("p o f -> p (o f)"), ACT.Copy).then_inc(act_done, 1)
                    act.activation(bg_now[:, :], bg[:, bass.ds(layer, 1)], ACT.Copy).then_inc(act_done, 1)
                    for n, (b, nb) in enumerate(GROUPS):
                        act.wait_ge(pe_done, n + 1)
                        act.activation(parts[:, 0, cols(b, nb)], bank[7][:, 0:nb * P], ACT.Copy).then_inc(relu1_done, 1)
                        act.wait_ge(y_done, n + 1)
                        act.activation(parts[:, 1, cols(b, nb)], part_left[:, n % 2, 0:nb * P], ACT.Copy).then_inc(relu1_done, 1)
                        for s in range(b, b + nb):
                            if s % 2 == 0:
                                convert(act, s, True)
                    for n, (b, nb) in enumerate(GROUPS):
                        act.wait_ge(dve_done, n + 1)
                        act.activation(h_fm[:, cols(b, nb)], agg[:, cols(b, nb)], ACT.Relu,
                                       bias=bg_now[:, 0:1]).then_inc(act_done, 1)

                @block.vector
                def _(dve):
                    for n, (b, nb) in enumerate(GROUPS):
                        dve.wait_ge(relu1_done, 2 * n + 1)
                        dve.tensor_tensor(part_left[:, n % 2, 0:nb * P], bank[7][:, 0:nb * P], parts[:, 0, cols(b, nb)],
                                          ALU.subtract).then_inc(y_done, 1)
                        dve.wait_ge(relu1_done, 2 * n + 2)
                        dve.tensor_tensor(parts[:, 2, cols(b, nb)], part_left[:, n % 2, 0:nb * P], parts[:, 1, cols(b, nb)],
                                          ALU.subtract).then_inc(relu2_done, 1)
                        for s in range(b, b + nb):
                            if s % 2 == 1:
                                convert(dve, s, False)
                    dve.wait_ge(block_used, 2 + BLOCKS)
                    for n, (b, nb) in enumerate(GROUPS):
                        dve.tensor_tensor(agg[:, cols(b, nb)], bank[n][:, 0:nb * P], dinv[:, cols(b, nb)],
                                          ALU.mult).then_inc(dve_done, 1)
                    for n, (b, nb) in enumerate(GROUPS):
                        dve.wait_ge(act_done, n + 3)
                        dve.tensor_tensor(h_fm[:, cols(b, nb)], h_fm[:, cols(b, nb)], dinv[:, cols(b, nb)], ALU.mult)

          with nc.Else():
            with phase("gcn_table") as block:
                @block.gpsimd
                def _(pool):
                    pool.memset(agg[:, NODES:COLS], 0.0)
                    split_on_pool(pool)

                @block.scalar
                def _(act):
                    act.activation(wg_now[:, :], wg[:, bass.ds(layer, 1), :].rearrange("p o f -> p (o f)"), ACT.Copy).then_inc(act_done, 1)
                    act.activation(bg_now[:, :], bg[:, bass.ds(layer, 1)], ACT.Copy)
                    for n, (b, nb) in enumerate(GROUPS):
                        act.wait_ge(pe_done, n + 1)
                        act.activation(stage[:, b:b + nb, :].rearrange("p b f -> p (b f)"), bank[n % 4][:, 0:nb * P],
                                       ACT.Copy).then_inc(relu1_done, 1)

                @block.tensor
                def _(pe):
                    pe.wait_ge(act_done, 1)
                    for n, (b, nb) in enumerate(GROUPS):
                        if n >= 4:
                            pe.wait_ge(relu1_done, n - 3)
                        for t in range(nb):
                            last = pe.matmul(bank[n % 4][:, t * P:(t + 1) * P], h_fm[:, cols(b + t, 1)], wg_now[:, :],
                                             start=True, stop=True)
                        last.then_inc(pe_done, 1)
                        if n >= 4:
                            pe.wait_ge(dve_done, n - 3)
                        pe.matmul(bank[4 + n % 4][:, 0:nb * P], wg_now[:, :], h_fm[:, cols(b, nb)],
                                  start=True, stop=True).then_inc(pe2_done, 1)

                @block.vector
                def _(dve):
                    for n, (b, nb) in enumerate(GROUPS):
                        dve.wait_ge(pe2_done, n + 1)
                        dve.tensor_copy(agg[:, cols(b, nb)], bank[4 + n % 4][:, 0:nb * P]).then_inc(dve_done, 1)

                @block.sync
                def _(sp):
                    for n, (b, nb) in enumerate(GROUPS):
                        sp.wait_ge(relu1_done, n + 1)
                        sp.dma_start(table[cols(b, nb), :].rearrange("(b p) f -> p b f", p=P),
                                     stage[:, b:b + nb, :]).then_inc(stored, 16)
                    sp.wait_ge(stored, 16 * NG)
                    split_on_sync(sp, layer)

            edge_passes("gcn", lambda block: edge_engines(block, agg, table, False), gather=True)

            with phase("gcn_act") as block:
                @block.vector
                def _(dve):
                    for n, (b, nb) in enumerate(GROUPS):
                        dve.tensor_tensor(agg[:, cols(b, nb)], agg[:, cols(b, nb)], dinv[:, cols(b, nb)],
                                          ALU.mult).then_inc(dve_done, 1)
                    for n, (b, nb) in enumerate(GROUPS):
                        dve.wait_ge(act_done, n + 1)
                        dve.tensor_tensor(h_fm[:, cols(b, nb)], h_fm[:, cols(b, nb)], dinv[:, cols(b, nb)], ALU.mult)

                @block.scalar
                def _(act):
                    for n, (b, nb) in enumerate(GROUPS):
                        act.wait_ge(dve_done, n + 1)
                        act.activation(h_fm[:, cols(b, nb)], agg[:, cols(b, nb)], ACT.Relu,
                                       bias=bg_now[:, 0:1]).then_inc(act_done, 1)

        with phase("gcn_out") as block:
            @block.sync
            def _(sp):
                sp.dma_start(x_nm[:, 0:XB, :], x[0:XB * P, :].rearrange("(b p) f -> p b f", p=P)).then_inc(loaded_x, 16)

            @block.scalar
            def _(act):
                for n, (b, nb) in enumerate(GROUPS):
                    act.activation(agg[:, cols(b, nb)], agg[:, cols(b, nb)], ACT.Identity,
                                   bias=bg_now[:, 0:1]).then_inc(act_done, 1)
                norm_act(act, x_nm, h_nm, ACT.Relu)

            @block.tensor
            def _(pe):
                for n, (b, nb) in enumerate(GROUPS):
                    pe.wait_ge(act_done, n + 1)
                    for t in range(nb):
                        last = pe.transpose(bank[n][:, t * P:(t + 1) * P], agg[:, cols(b + t, 1)], ident[:, :])
                    last.then_inc(pe_done, 1)
                pe.wait_ge(pe3_done, 1)
                to_feature_major(pe)

            @block.vector
            def _(dve):
                link = Chain(dve, dve_done)
                dve.wait_ge(loaded_x, 16)
                for n, (b, nb) in enumerate(GROUPS):
                    dve.wait_ge(pe_done, n + 1)
                    ins = dve.tensor_tensor(x_nm[:, b:b + nb, :].rearrange("p b f -> p (b f)"),
                                            x_nm[:, b:b + nb, :].rearrange("p b f -> p (b f)"), bank[n][:, 0:nb * P], ALU.add)
                link(ins)
                dve.sem_inc(pe3_done, 1)
                norm_dve(dve, link, x_nm)
                for n, (b, nb) in enumerate(GROUPS):
                    dve.wait_ge(pe2_done, n + 1)
                    dve.tensor_copy(h_fm[:, cols(b, nb)], bank[n][:, 0:nb * P])

        with nc.Fori(0, STEPS) as _step:
            with phase("mp_table") as block:
                def part_of(half, part, b, nb):
                    return src_stage[:, b:b + nb, part, :] if half == 0 else dst_stage[:, part, b:b + nb, :]

                def work():
                    for m in range(2 * NG):
                        b, nb = GROUPS[m // 2]
                        yield m, m % 2, b, nb, bank[m % 8][:, 0:nb * P].rearrange("p (b f) -> p b f", f=P), \
                            left_over[:, m % 4, 0:nb * P].rearrange("p (b f) -> p b f", f=P)

                @block.tensor
                def _(pe):
                    for m, half, b, nb, _, _ in work():
                        if m >= 8:
                            pe.wait_ge(dve_done, m - 7)
                        for t in range(nb):
                            last = pe.matmul(bank[m % 8][:, t * P:(t + 1) * P], h_fm[:, cols(b + t, 1)],
                                             w1ab[:, half * P:(half + 1) * P], start=True, stop=True)
                        last.then_inc(pe_done, 1)

                @block.scalar
                def _(act):
                    def second(m):
                        b, nb = GROUPS[m // 2]
                        act.wait_ge(dve_done, m + 1)
                        act.activation(part_of(m % 2, 1, b, nb),
                                       left_over[:, m % 4, 0:nb * P].rearrange("p (b f) -> p b f", f=P),
                                       ACT.Copy).then_inc(relu2_done, 1)

                    for m, half, b, nb, sums, _ in work():
                        act.wait_ge(pe_done, m + 1)
                        act.activation(part_of(half, 0, b, nb), sums, ACT.Copy).then_inc(relu1_done, 1)
                        if m >= 1:
                            second(m - 1)
                    second(2 * NG - 1)

                @block.vector
                def _(dve):
                    for m, half, b, nb, sums, left_of in work():
                        dve.wait_ge(relu1_done, m + 1)
                        if m >= 4:
                            dve.wait_ge(pool_done, m - 3)
                        dve.tensor_tensor(left_of, sums, part_of(half, 0, b, nb), ALU.subtract).then_inc(dve_done, 1)

                @block.gpsimd
                def _(pool):
                    for m, half, b, nb, _, left_of in work():
                        pool.wait_ge(relu2_done, m + 1)
                        pool.tensor_tensor(part_of(half, 2, b, nb), left_of, part_of(half, 1, b, nb),
                                           ALU.subtract).then_inc(pool_done, 1)
                    pool.memset(agg[:, :], 0.0)

                @block.sync
                def _(sp):
                    for n, (b, nb) in enumerate(GROUPS):
                        sp.wait_ge(pool_done, 2 * n + 1)
                        sp.dma_start(src_table[cols(b, nb), :].rearrange("(b p) f -> p b f", p=P),
                                     src_stage[:, b:b + nb, :, :].rearrange("p b s f -> p b (s f)")).then_inc(stored, 16)
                        sp.wait_ge(pool_done, 2 * n + 2)
                        for part in range(3):
                            sp.dma_start(dst_table[part, cols(b, nb), :].rearrange("(b p) f -> p b f", p=P),
                                         dst_stage[:, part, b:b + nb, :]).then_inc(stored, 16)
                    sp.wait_ge(stored, 64 * NG)

            edge_passes("mp", lambda block: edge_engines(block, agg, src_table, True), gather=True)

            with phase("update") as block:
                def stages(run):
                    for n in range(NG + 3):
                        for s in range(4):
                            if 0 <= n - s < NG:
                                run(s, n - s, *GROUPS[n - s])

                @block.tensor
                def _(pe):
                    def run(s, n, b, nb):
                        c = nb * P
                        to = bank[2 * s + n % 2]
                        if s == 0:
                            if n >= 2:
                                pe.wait_ge(third_done, n - 1)
                            pe.matmul(to[:, 0:c], w3[:, :], agg[:, cols(b, nb)], start=True, stop=True).then_inc(sums3_done, 1)
                        elif s == 1:
                            if n >= 2:
                                pe.wait_ge(hidden1_done, n - 1)
                            pe.matmul(to[:, 0:c], u1a[:, :], h_fm[:, cols(b, nb)], start=True, stop=False)
                            pe.wait_ge(third_done, n + 1)
                            pe.matmul(to[:, 0:c], u1b[:, :], t1[:, n % 2, 0:c], start=False, stop=True).then_inc(y_done, 1)
                        elif s == 2:
                            pe.wait_ge(hidden1_done, n + 1)
                            if n >= 2:
                                pe.wait_ge(hidden2_done, n - 1)
                            pe.matmul(to[:, 0:c], u2[:, :], t2[:, n % 2, 0:c], start=True, stop=True).then_inc(counted, 1)
                        else:
                            pe.wait_ge(hidden2_done, n + 1)
                            if n >= 2:
                                pe.wait_ge(updated, n - 1)
                            for t in range(nb):
                                last = pe.matmul(to[:, t * P:(t + 1) * P], t2[:, 2 + n % 2, t * P:(t + 1) * P], u3[:, :],
                                                 start=True, stop=True)
                            last.then_inc(pe_done, 1)

                    stages(run)
                    pe.wait_ge(updated, NG)
                    to_feature_major(pe)

                @block.gpsimd
                def _(pool):
                    for n, (b, nb) in enumerate(GROUPS):
                        pool.tensor_tensor(h_nm[:, b:b + nb, :], h_nm[:, b:b + nb, :],
                                           c3_row[:, :].unsqueeze(1).to_broadcast([P, nb, P]), ALU.add).then_inc(pool_done, 1)
                    for n, (b, nb) in enumerate(GROUPS):
                        pool.wait_ge(gained, n + 1)
                        pool.tensor_tensor(h_nm[:, b:b + nb, :], h_nm[:, b:b + nb, :],
                                           be_row[:, :].unsqueeze(1).to_broadcast([P, nb, P]), ALU.add).then_inc(relu2_done, 1)

                @block.vector
                def _(dve):
                    link = Chain(dve, dve_done)

                    def run(s, n, b, nb):
                        c = nb * P
                        if s == 0:
                            dve.wait_ge(sums3_done, n + 1)
                            if n >= 2:
                                dve.wait_ge(y_done, n - 1)
                            dve.scalar_tensor_tensor(out=t1[:, n % 2, 0:c], in0=deg[:, cols(b, nb)], scalar=b3_col[:, 0:1],
                                                     in1=bank[n % 2][:, 0:c], op0=ALU.mult, op1=ALU.add).then_inc(third_done, 1)
                        elif s == 3:
                            dve.wait_ge(pool_done, n + 1)
                            dve.wait_ge(pe_done, n + 1)
                            h2 = h_nm[:, b:b + nb, :].rearrange("p b f -> p (b f)")
                            dve.tensor_tensor(h2, h2, bank[6 + n % 2][:, 0:c], ALU.add).then_inc(updated, 1)
                            dve.wait_ge(updated, n + 1)
                            for t in range(b, b + nb):
                                ins = dve.bn_stats(stats[:, t, :], h_nm[:, t, :])
                            link(ins)
                            for t in range(b, b + nb):
                                ins = dve.bn_aggr(mv[:, t, :], stats[:, t, :])
                            ins.then_inc(z_done, 1)

                    stages(run)
                    dve.wait_ge(rooted, 1)
                    link(dve.reciprocal(rstd[:, :], rstd[:, :]))
                    dve.scalar_tensor_tensor(out=shift[:, :], in0=mv[:, :, 0], scalar=-1.0, in1=rstd[:, :],
                                             op0=ALU.mult, op1=ALU.mult).then_inc(relu1_done, 1)
                    for n, (b, nb) in enumerate(GROUPS):
                        dve.wait_ge(onehot_t_ready, n + 1)
                        h3 = h_nm[:, b:b + nb, :]
                        dve.tensor_tensor(h3, h3, g_row[:, :].unsqueeze(1).to_broadcast([P, nb, P]), ALU.mult).then_inc(gained, 1)
                    for n, (b, nb) in enumerate(GROUPS):
                        dve.wait_ge(pe2_done, n + 1)
                        dve.tensor_copy(h_fm[:, cols(b, nb)], bank[n][:, 0:nb * P])

                @block.scalar
                def _(act):
                    def run(s, n, b, nb):
                        c = nb * P
                        if s == 1:
                            act.wait_ge(y_done, n + 1)
                            if n >= 2:
                                act.wait_ge(counted, n - 1)
                            act.activation(t2[:, n % 2, 0:c], bank[2 + n % 2][:, 0:c], ACT.Relu,
                                           bias=c1_col[:, 0:1]).then_inc(hidden1_done, 1)
                        elif s == 2:
                            act.wait_ge(counted, n + 1)
                            if n >= 2:
                                act.wait_ge(pe_done, n - 1)
                            act.activation(t2[:, 2 + n % 2, 0:c], bank[4 + n % 2][:, 0:c], ACT.Relu,
                                           bias=c2_col[:, 0:1]).then_inc(hidden2_done, 1)

                    stages(run)
                    act.wait_ge(z_done, NG)
                    act.activation(rstd[:, :], mv[:, :, 1], ACT.Sqrt, bias=eps_col[:, 0:1]).then_inc(rooted, 1)
                    act.wait_ge(relu1_done, 1)
                    for b, nb in GROUPS:
                        for t in range(b, b + nb):
                            ins = act.activation(h_nm[:, t, :], h_nm[:, t, :], ACT.Identity, bias=shift[:, t:t + 1],
                                                 scale=rstd[:, t:t + 1])
                        ins.then_inc(onehot_t_ready, 1)

        with phase("output") as block:
            @block.vector
            def _(dve):
                dve.tensor_tensor(x_nm[:, :, :], x_nm[:, :, :], h_nm[:, :, :], ALU.add).then_inc(dve_done, 1)

            @block.sync
            def _(sp):
                sp.wait_ge(dve_done, 1)
                sp.dma_start(out[0:FULL * P, :].rearrange("(b p) f -> p b f", p=P), x_nm[:, 0:FULL, :]).then_inc(stored, 16)
                sp.dma_start(out[FULL * P:N, :], x_nm[0:REST, FULL, :]).then_inc(stored, 16)
                sp.wait_ge(stored, 32)


def kernel(**inputs):
    import numpy as np
    import concourse.bacc as bacc
    from concourse.bass_utils import run_bass_kernel_spmd

    a = {k: np.asarray(v) for k, v in inputs.items()}
    n, d = a["x"].shape
    edges = a["src"].shape[0]
    group = SLOTS * CHUNK
    padded = -(-edges // group) * group
    src = np.zeros(padded, a["src"].dtype)
    src[:edges] = a["src"]
    dst = np.full(padded, n, a["dst"].dtype)
    dst[:edges] = a["dst"]
    features = a["edge_attr_32"].shape[1]
    edge_t = np.zeros((features, padded), a["edge_attr_32"].dtype)
    edge_t[:, :edges] = a["edge_attr_32"].T
    quarters = P // features
    edge_q = edge_t.reshape(features, quarters, -1).transpose(1, 0, 2).reshape(P, -1)
    arrays = {
        "x": a["x"],
        "src_pt": np.ascontiguousarray(src.reshape(-1, P).T),
        "dst_pt": np.ascontiguousarray(dst.reshape(-1, P).T),
        "dst_flat": dst,
        "edge_q": np.ascontiguousarray(edge_q),
    }
    groups = {
        "w_gcn": [f"L0_gnn_W{i}" for i in (1, 2, 3)], "b_gcn": [f"L0_gnn_b{i}" for i in (1, 2, 3)],
        "msg_w": [f"L1_gnn_msg_w{i}" for i in (1, 2, 3)], "msg_b": [f"L1_gnn_msg_b{i}" for i in (1, 2, 3)],
        "upd_w": [f"L1_gnn_upd_w{i}" for i in (1, 2, 3)], "upd_b": [f"L1_gnn_upd_b{i}" for i in (1, 2, 3)],
    }
    for names in groups.values():
        arrays |= {name: a[name] for name in names}
    arrays |= {"ln_g": a["L1_gnn_ln_g"], "ln_b": a["L1_gnn_ln_b"]}

    nc = bacc.Bacc("TRN2", target_bir_lowering=False, num_devices=1)
    aps = {k: nc.dram_tensor(f"in_{k}", v.shape, mybir.dt.from_np(v.dtype), kind="ExternalInput").ap()
           for k, v in arrays.items()}
    out = nc.dram_tensor("out", (n, d), F32, kind="ExternalOutput").ap()
    gnn_program(nc, aps["x"], aps["src_pt"], aps["dst_pt"], aps["dst_flat"], aps["edge_q"],
                *([aps[name] for name in names] for names in groups.values()), aps["ln_g"], aps["ln_b"], out)
    r = run_bass_kernel_spmd(nc, [{f"in_{k}": v for k, v in arrays.items()}], core_ids=[0])
    return r.results[0]["out"]
```

```python
from contextlib import ExitStack, contextmanager

import concourse.bass as bass
from concourse import mybir

F32 = mybir.dt.float32
BF16 = mybir.dt.bfloat16
I16 = mybir.dt.int16
U8 = mybir.dt.uint8
I32 = mybir.dt.int32
U32 = mybir.dt.uint32
ALU = mybir.AluOpType
ACT = mybir.ActivationFunctionType
AX = mybir.AxisListType

P = 128
TPC = 4
CHUNK = TPC * P
SLOTS = 4
WIN = 39
CWIN = 44
DENSE_MAX = 120
EPS = 1e-5


def gnn_program(nc, x, src_pt, dst_pt, dst_flat, edge_q, w_gcn, b_gcn, msg_w, msg_b, upd_w, upd_b, ln_g, ln_b, out):
    N = x.shape[0]
    TILES = src_pt.shape[1]
    CHUNKS = TILES // TPC
    ITERS = CHUNKS // SLOTS
    QUARTERS = 4
    ED = P // QUARTERS
    QCOLS = edge_q.shape[1]
    SPLIT = 1024
    BLOCKS = -(-N // P)
    NODES = BLOCKS * P
    FULL = N // P
    REST = N - FULL * P
    COLS = NODES + CWIN
    GB = TPC
    GROUPS = [(b, min(GB, BLOCKS - b)) for b in range(0, BLOCKS, GB)]
    NG = len(GROUPS)
    MAXPASS = -(-(NODES + 1) // WIN)
    LAYERS = len(w_gcn)
    STEPS = 3
    TB = -(-BLOCKS // 3)
    THIRDS = [(b, min(TB, BLOCKS - b)) for b in range(0, BLOCKS, TB)]
    KEYS = BLOCKS * CWIN
    assert TB * CWIN <= CHUNK and COLS % 4 == 0 and CWIN % 4 == 0 and CWIN >= WIN + 3
    SRC_ON_DVE = 2
    ROUNDS = QCOLS // SPLIT
    LAYER_STEP = -(-(ROUNDS - 1) // LAYERS)
    assert QCOLS % SPLIT == 0 and LAYER_STEP * LAYERS + 1 == ROUNDS

    with ExitStack() as ctx:
        def sb(name, shape, dt=F32):
            return ctx.enter_context(nc.sbuf_tensor(name, shape, dt))

        def sem(name):
            return ctx.enter_context(nc.semaphore(name))

        def cols(b, nb):
            return slice(b * P, (b + nb) * P)

        table = nc.dram_tensor("table", [NODES, P], F32).ap()
        src_table = nc.dram_tensor("src_table", [NODES, 3 * P], BF16).ap()
        dst_table = nc.dram_tensor("dst_table", [3, COLS, P], BF16).ap()
        edge_table = nc.dram_tensor("edge_table", [3 * ED, QUARTERS * QCOLS], BF16).ap()
        dst_short = nc.dram_tensor("dst_short", [CHUNKS, CHUNK], I16).ap()

        bank = [ctx.enter_context(nc.psum_tensor(f"bank{i}", [P, CHUNK], F32)) for i in range(8)]

        wg = sb("wg", [P, LAYERS, P])
        wg_now = sb("wg_now", [P, P])
        bg = sb("bg", [P, LAYERS])
        bg_now = sb("bg_now", [P, 1])
        w1ab = sb("w1ab", [P, 2 * P])
        w1c = sb("w1c", [3 * ED, P])
        w1c_parts = sb("w1c_parts", [3 * ED, 3, P], BF16)
        w2 = sb("w2", [P, P])
        w3 = sb("w3", [P, P])
        u1a = sb("u1a", [P, P])
        u1b = sb("u1b", [P, P])
        u2 = sb("u2", [P, P])
        u3 = sb("u3", [P, P])
        b1_col = sb("b1_col", [P, 1])
        b3_col = sb("b3_col", [P, 1])
        w3u1b = sb("w3u1b", [P, P])
        b3u1b_col = sb("b3u1b_col", [P, 1])
        c1_col = sb("c1_col", [P, 1])
        c2_col = sb("c2_col", [P, 1])
        c3_row = sb("c3_row", [P, P])
        g_row = sb("g_row", [P, P])
        be_row = sb("be_row", [P, P])
        b2_rep = sb("b2_rep", [3, P])
        b2_left = sb("b2_left", [3, 2, P])
        b2_part = sb("b2_part", [3, 3, P], BF16)
        b2_split = sb("b2_split", [3, TPC, P], BF16)
        ones_bf = sb("ones_bf", [3, P], BF16)
        ones = sb("ones", [P, P])
        ident = sb("ident", [P, P])
        eps_col = sb("eps_col", [P, 1])
        win_i = sb("win_i", [P, WIN], I32)
        win_iota = sb("win_iota", [P, WIN])
        part_i = sb("part_i", [P, 1], I32)
        part_iota = sb("part_iota", [P, 1])
        step_i = sb("step_i", [P, MAXPASS], I32)
        steps_f = sb("steps_f", [P, MAXPASS])
        key_iota = sb("key_iota", [P, KEYS], I16)
        node_iota = sb("node_iota", [P, P])
        ones_b = sb("ones_b", [P, P], BF16)
        ident_b = sb("ident_b", [P, P], BF16)

        src_sb = sb("src_sb", [P, TILES], I32)
        dst_sb = sb("dst_sb", [P, TILES], I32)
        dst_f = sb("dst_f", [P, TILES])
        dst_rows = sb("dst_rows", [CHUNKS, CHUNK], I32)
        lo_hi = sb("lo_hi", [CHUNKS, 2])
        diag = sb("diag", [CHUNKS, 2, CHUNKS])
        lo_all = sb("lo_all", [P, CHUNKS])
        span = sb("span", [P, CHUNKS])
        span_max = sb("span_max", [P, 1])
        over = sb("over", [P, MAXPASS])
        pass_f = sb("pass_f", [P, 1])
        pass_i = sb("pass_i", [P, 1], I32)
        pass_off = sb("pass_off", [P, 1])
        win_lo = sb("win_lo", [P, CHUNKS])
        win_lo_i = sb("win_lo_i", [P, CHUNKS], I32)
        win_word = sb("win_word", [P, CHUNKS], I32)
        win_shift = sb("win_shift", [P, CHUNKS])
        rel = sb("rel", [P, TILES])
        src_place = sb("src_place", [P, TILES])
        src_neg = sb("src_neg", [P, TILES])
        src_block = sb("src_block", [P, TILES])
        key = sb("key", [P, TILES])
        deg_max = sb("deg_max", [P, 1])
        sparse_i = sb("sparse_i", [P, 1], I32)
        win_node = sb("win_node", [3 * WIN, CHUNKS])
        part_node = sb("part_node", [P, 1])
        dst_rows_s = sb("dst_rows_s", [CHUNKS, CHUNK], I16)

        x_nm = sb("x_nm", [P, BLOCKS, P])
        h_nm = sb("h_nm", [P, BLOCKS, P])
        h_fm = sb("h_fm", [P, NODES])
        wide = sb("wide", [P, 3 * NODES // 2])
        agg = wide[:, 0:COLS]
        parts = wide[:, :].bitcast(BF16).rearrange("p (b s f) -> p b s f", s=3, f=P)
        assert COLS * 4 <= (BLOCKS - 2) * 3 * P * 2
        deg = sb("deg", [P, COLS])
        dinv = sb("dinv", [P, NODES])
        shared = sb("shared", [P, BLOCKS * COLS // 4])
        counts = shared[:, :].bitcast(U8).rearrange("p (b c) -> p b c", c=COLS)
        used = 0

        def carve(shape, dt=F32):
            nonlocal used
            size = 4
            n = 1
            for d in shape[1:]:
                n *= d
            size = n * {F32: 4, I32: 4, BF16: 2, I16: 2}[dt] // 4
            part = shared[0:shape[0], used:used + size].bitcast(dt)
            used += size
            assert used <= BLOCKS * COLS // 4
            names = "abc"[:len(shape) - 1]
            dims = {c: d for c, d in zip(names[1:], shape[2:])}
            return part.rearrange(f"p ({' '.join(names)}) -> p {' '.join(names)}", **dims) if len(names) > 1 else part

        part_left = sb("part_left", [P, 2, CHUNK])
        counts_bf = h_nm[:, :, :].rearrange("p b f -> p (b f)").bitcast(BF16).rearrange("p (s n) -> p s n", s=2)
        key_onehot = wide[:, :].bitcast(BF16)[:, 0:2 * TPC * KEYS].rearrange(
            "p (s t k) -> p s t k", s=2, t=TPC)
        left = part_left[:, :, :].rearrange("p s n -> p (s n)")
        inside = left[:, 0:2 * TILES].rearrange("p (s t) -> p s t", s=2)
        key_i = wide[:, 0:KEYS].bitcast(I32)
        src_i = wide[:, KEYS:KEYS + TILES].bitcast(I32)
        low_bits = wide[:, 0:CHUNKS].bitcast(I32)
        squares = counts_bf[:, :, :].rearrange("p s n -> p (s n)").bitcast(F32)[:, 0:2 * TPC * P].rearrange(
            "p (s t r) -> p s t r", s=2, t=TPC)
        win_onehot = left[:, 0:TPC * WIN].bitcast(BF16).rearrange(
            "p (s t w) -> p s t w", s=2, t=TPC)
        src_onehot = left[:, TPC * WIN:TPC * (WIN + P)].bitcast(BF16).rearrange(
            "p (s t r) -> p s t r", s=2, t=TPC)
        sum_words = h_nm[:, BLOCKS - 5:BLOCKS, :].rearrange("p b f -> p (b f)").bitcast(I32)[:, 0:2 * KEYS // 4].rearrange(
            "p (s b w) -> p s b w", s=2, b=BLOCKS)
        sum_bytes = h_nm[:, BLOCKS - 5:BLOCKS, :].rearrange("p b f -> p (b f)").bitcast(U8)[:, 0:2 * KEYS].rearrange(
            "p (s k) -> p s k", s=2)
        count_words = shared[:, :].bitcast(I32).rearrange("p (b c) -> p b c", c=COLS // 4)
        dinv_nm = left[:, 0:BLOCKS]
        w3_turned = left[:, P:2 * P]
        dinv_diag = h_nm
        stats = sb("stats", [P, BLOCKS, 6])
        mv = sb("mv", [P, BLOCKS, 2])
        rstd = sb("rstd", [P, BLOCKS])
        shift = sb("shift", [P, BLOCKS])

        idx = sb("idx", [P, SLOTS * TPC], I32)
        rows_b = carve([P, SLOTS * TPC, 3 * P], BF16)
        rows = rows_b[:, :, :].rearrange("p j f -> p (j f)")[:, 0:2 * SLOTS * TPC * P].bitcast(F32).rearrange(
            "p (j f) -> p j f", f=P)
        onehot = carve([P, SLOTS, TPC, WIN])
        onehot_t = carve([3 * WIN, SLOTS, CHUNK], BF16)
        dst_bc = carve([3 * WIN, SLOTS, CHUNK], I16)
        dst_win = carve([3 * WIN, SLOTS, P], BF16)
        edge_in = carve([3 * ED, SLOTS, CHUNK], BF16)
        r1 = carve([P, 2, CHUNK])
        r2 = carve([P, SLOTS, CHUNK])

        edge_words = used
        used = 0
        stage = carve([P, BLOCKS, P])
        used = 0
        src_stage = carve([P, BLOCKS, 3 * P], BF16).rearrange("p b (s f) -> p b s f", s=3)
        dst_stage = carve([P, 3 * BLOCKS, P], BF16).rearrange("p (s b) f -> p s b f", s=3)
        left_over = carve([P, 4, CHUNK])
        t2 = carve([P, 4, CHUNK])
        assert used >= edge_words and BLOCKS == ITERS - 1
        hidden = carve([P, NODES])
        XB = 5 * SPLIT // 2 // P
        x_flat = x_nm[:, 0:XB, :].rearrange("p b f -> p (b f)")
        feat = x_flat[:, 0:SPLIT]
        feat_parts = x_flat[:, SPLIT:5 * SPLIT // 2].bitcast(BF16).rearrange("p (s n) -> p s n", s=3)
        assert XB <= FULL

        loaded = sem("loaded")
        loaded_idx = sem("loaded_idx")
        loaded_x = sem("loaded_x")
        pool_done = sem("pool_done")
        dve_done = sem("dve_done")
        act_done = sem("act_done")
        pe_done = sem("pe_done")
        pe2_done = sem("pe2_done")
        stored = sem("stored")
        idx_ready = sem("idx_ready")
        onehot_ready = sem("onehot_ready")
        onehot_t_ready = sem("onehot_t_ready")
        seg_done = sem("seg_done")
        window_added = sem("window_added")
        z_done = sem("z_done")
        gathers_begun = sem("gathers_begun")
        relu1_done = sem("relu1_done")
        y_done = sem("y_done")
        relu2_done = sem("relu2_done")
        dst_bc_in = [sem(f"dst_bc_in{k}") for k in range(SLOTS)]
        dst_win_in = [sem(f"dst_win_in{k}") for k in range(SLOTS)]
        edge_in_in = [sem(f"edge_in_in{k}") for k in range(SLOTS)]
        keys_ready = sem("keys_ready")
        counted = sem("counted")
        degrees_counted = sem("degrees_counted")
        degrees_added = sem("degrees_added")
        sums_copied = sem("sums_copied")
        squared = sem("squared")
        hidden1_summed = sem("hidden1_summed")
        relued = sem("relued")
        hidden1_done = sem("hidden1_done")
        hidden2_done = sem("hidden2_done")
        updated = sem("updated")
        biased = sem("biased")
        sums_read = sem("sums_read")
        product1_done = sem("product1_done")
        product2_done = sem("product2_done")
        product3_done = sem("product3_done")
        sampled = sem("sampled")
        measured = sem("measured")
        rooted = sem("rooted")
        inverted = sem("inverted")
        shifted = sem("shifted")
        normalised = sem("normalised")
        rows_ready = sem("rows_ready")
        turned = sem("turned")
        columns_ready = sem("columns_ready")
        products_ready = sem("products_ready")
        first_parts = sem("first_parts")
        left_ready = sem("left_ready")
        second_parts = sem("second_parts")
        third_parts = sem("third_parts")
        gained = sem("gained")
        feat_in = sem("feat_in")
        feat_split = sem("feat_split")
        split_begun = sem("split_begun")
        feat_stored = sem("feat_stored")
        block_ready = [sem(f"block_ready{n}") for n in range(2)]
        block_used = sem("block_used")
        gathered = [sem(f"gathered{j}") for j in range(SLOTS * TPC)]
        all_sems = [loaded, loaded_idx, loaded_x, pool_done, dve_done, act_done, pe_done, pe2_done, stored,
                    idx_ready, onehot_ready, onehot_t_ready, seg_done, window_added, gathers_begun, z_done, relu1_done, y_done,
                    relu2_done, keys_ready, counted, degrees_counted, degrees_added, sums_copied, squared, hidden1_summed, relued, hidden1_done, hidden2_done, updated, biased, sums_read, product1_done, product2_done, product3_done, sampled, measured, rooted, inverted, shifted, normalised, rows_ready, turned, columns_ready, products_ready, first_parts, left_ready, second_parts, third_parts, gained, feat_in, feat_split, split_begun, feat_stored, *block_ready, block_used, *dst_bc_in, *dst_win_in, *edge_in_in, *gathered]
        nums = sorted(s.num for s in all_sems)
        assert nums == list(range(nums[0], nums[-1] + 1))
        gathers = sorted(s.num for s in gathered)

        @contextmanager
        def phase(name, gather=False):
            with nc.Block(name) as block:
                yield block
            if gather:
                nc.gpsimd.dma_reset(range(gathers[0], gathers[-1] + 1))
            nc.all_engine_barrier(sems_to_clear=range(nums[0], nums[-1] + 1))

        class Chain:

            def __init__(self, eng, s):
                self.eng, self.s, self.n = eng, s, 0

            def __call__(self, ins):
                self.n += 1
                ins.then_inc(self.s, 1)
                self.eng.wait_ge(self.s, self.n)

        def node_stages(made, rows_from, gain=False, tables=False, final=False):
            turn = made + (5 if gain else 3)
            return {"made": made, "from": rows_from, "gain": gain, "tables": tables, "final": final,
                    "norm": made + 2, "gained": made + 3, "turn": turn, "split": turn + 1,
                    "last": turn + 1 if tables else turn}

        def rounds(nodes, *stages):
            for r in range(NG + nodes["last"]):
                for at, run in stages:
                    if 0 <= r - at < NG:
                        run(r - at, *GROUPS[r - at])

        def nodes_on_dve(nodes, dve, *head):
            def shift_of(n, b, nb):
                dve.wait_ge(rooted, n + 1)
                dve.reciprocal(rstd[:, b:b + nb], rstd[:, b:b + nb]).then_inc(inverted, 1)
                dve.wait_ge(inverted, n + 1)
                dve.scalar_tensor_tensor(out=shift[:, b:b + nb], in0=mv[:, b:b + nb, 0], scalar=-1.0, in1=rstd[:, b:b + nb],
                                         op0=ALU.mult, op1=ALU.mult).then_inc(shifted, 1)

            def gain_of(n, b, nb):
                dve.wait_ge(normalised, n + 1)
                h = h_nm[:, b:b + nb, :]
                dve.tensor_tensor(h, h, g_row[:, :].unsqueeze(1).to_broadcast([P, nb, P]), ALU.mult).then_inc(gained, 1)

            def copy_columns(n, b, nb):
                dve.wait_ge(turned, n + 1)
                dve.tensor_copy(h_fm[:, cols(b, nb)], bank[4][:, 0:nb * P]).then_inc(columns_ready, 1)

            def add_x(n, b, nb):
                dve.wait_ge(rows_ready, n + 1)
                x_of = x_nm[:, b:b + nb, :]
                dve.tensor_tensor(x_of, x_of, h_nm[:, b:b + nb, :], ALU.add).then_inc(columns_ready, 1)

            def left_of(n, b, nb):
                for half in range(2):
                    m = 2 * n + half
                    dve.wait_ge(first_parts, m + 1)
                    if m >= 4:
                        dve.wait_ge(third_parts, m - 3)
                    dve.tensor_tensor(group(left_over[:, m % 4, 0:nb * P]), group(bank[5 + half][:, 0:nb * P]),
                                      part_of(half, 0, b, nb), ALU.subtract).then_inc(left_ready, 1)

            rounds(nodes, (nodes["norm"], shift_of), *[(nodes["gained"], gain_of)] * nodes["gain"],
                        (nodes["turn"], add_x if nodes["final"] else copy_columns),
                        *[(nodes["split"], left_of)] * nodes["tables"], *head)

        def measure(nodes, dve, n, b, nb):
            for t in range(b, b + nb):
                ins = dve.bn_stats(stats[:, t, :], nodes["from"][:, t, :])
            ins.then_inc(sampled, 1)
            dve.wait_ge(sampled, n + 1)
            for t in range(b, b + nb):
                ins = dve.bn_aggr(mv[:, t, :], stats[:, t, :])
            ins.then_inc(measured, 1)

        def nodes_on_act(nodes, act, *head):
            def normalise(n, b, nb):
                act.wait_ge(shifted, n + 1)
                for t in range(b, b + nb):
                    ins = act.activation(h_nm[:, t, :], nodes["from"][:, t, :], ACT.Identity if nodes["gain"] else ACT.Relu,
                                         bias=shift[:, t:t + 1], scale=rstd[:, t:t + 1])
                ins.then_inc(normalised if nodes["gain"] else rows_ready, 1)

            def parts_of(n, b, nb):
                for half in range(2):
                    act.wait_ge(products_ready, 2 * n + half + 1)
                    act.activation(part_of(half, 0, b, nb), group(bank[5 + half][:, 0:nb * P]), ACT.Copy).then_inc(first_parts, 1)
                for half in range(2):
                    m = 2 * n + half
                    act.wait_ge(left_ready, m + 1)
                    act.activation(part_of(half, 1, b, nb), group(left_over[:, m % 4, 0:nb * P]), ACT.Copy).then_inc(second_parts, 1)

            def root(n, b, nb):
                act.wait_ge(measured, n + 1)
                act.activation(rstd[:, b:b + nb], mv[:, b:b + nb, 1], ACT.Sqrt, bias=eps_col[:, 0:1]).then_inc(rooted, 1)

            rounds(nodes, (nodes["norm"], normalise), *[(nodes["split"], parts_of)] * nodes["tables"], *head, (nodes["made"], root))

        def nodes_on_pool(nodes, pool, *head):
            def shift_rows(n, b, nb):
                pool.wait_ge(gained, n + 1)
                pool.tensor_tensor(h_nm[:, b:b + nb, :], h_nm[:, b:b + nb, :],
                                   be_row[:, :].unsqueeze(1).to_broadcast([P, nb, P]), ALU.add).then_inc(rows_ready, 1)

            def third(n, b, nb):
                for half in range(2):
                    m = 2 * n + half
                    pool.wait_ge(second_parts, m + 1)
                    pool.tensor_tensor(part_of(half, 2, b, nb), group(left_over[:, m % 4, 0:nb * P]),
                                       part_of(half, 1, b, nb), ALU.subtract).then_inc(third_parts, 1)

            def clear(n, b, nb):
                if n == 0:
                    pool.wait_ge(sums_read, NG)
                    pool.memset(agg[:, :], 0.0)

            rounds(nodes, *[(nodes["gained"], shift_rows)] * nodes["gain"], *[(nodes["split"], third), (NG, clear)] * nodes["tables"], *head)

        def nodes_on_pe(nodes, pe, *head):
            def turn(n, b, nb):
                pe.wait_ge(rows_ready, n + 1)
                if n >= 1:
                    pe.wait_ge(columns_ready, n)
                for t in range(nb):
                    last = pe.transpose(bank[4][:, t * P:(t + 1) * P], h_nm[:, b + t, :], ident[:, :])
                last.then_inc(turned, 1)

            def products(n, b, nb):
                pe.wait_ge(columns_ready, n + 1)
                for half in range(2):
                    if n >= 1:
                        pe.wait_ge(left_ready, 2 * n + half - 1)
                    for t in range(nb):
                        last = pe.matmul(bank[5 + half][:, t * P:(t + 1) * P], h_fm[:, cols(b + t, 1)],
                                         w1ab[:, half * P:(half + 1) * P], start=True, stop=True)
                    last.then_inc(products_ready, 1)

            rounds(nodes, *[(nodes["turn"], turn)] * (not nodes["final"]), *[(nodes["split"], products)] * nodes["tables"], *head)

        def nodes_on_sync(nodes, sp):
            if nodes["tables"]:
                for n, (b, nb) in enumerate(GROUPS):
                    sp.wait_ge(third_parts, 2 * n + 1)
                    sp.dma_start(src_table[cols(b, nb), :].rearrange("(b p) f -> p b f", p=P),
                                 src_stage[:, b:b + nb, :, :].rearrange("p b s f -> p b (s f)")).then_inc(stored, 16)
                    sp.wait_ge(third_parts, 2 * n + 2)
                    for part in range(3):
                        sp.dma_start(dst_table[part, cols(b, nb), :].rearrange("(b p) f -> p b f", p=P),
                                     dst_stage[:, part, b:b + nb, :]).then_inc(stored, 16)
                sp.wait_ge(stored, 64 * NG)
            if nodes["final"]:
                for n, (b, nb) in enumerate(GROUPS):
                    sp.wait_ge(columns_ready, n + 1)
                    whole = min(nb, FULL - b)
                    if whole:
                        sp.dma_start(out[cols(b, whole), :].rearrange("(b p) f -> p b f", p=P),
                                     x_nm[:, b:b + whole, :]).then_inc(stored, 16)
                sp.dma_start(out[FULL * P:N, :], x_nm[0:REST, FULL, :]).then_inc(stored, 16)
                sp.wait_ge(stored, 16 * (sum(b < FULL for b, _ in GROUPS) + 1))

        def part_of(half, part, b, nb):
            return src_stage[:, b:b + nb, part, :] if half == 0 else dst_stage[:, part, b:b + nb, :]

        def group(columns):
            return columns.rearrange("p (b f) -> p b f", f=P)

        WEIGHT_LOADS = 2 * LAYERS + 19
        DIAG_STEPS = 4
        rows_in = node_stages(0, x_nm)
        with phase("load") as block:
            @block.sync
            def _(sp):
                sp.dma_start(dst_rows[:, :], dst_flat.rearrange("(c e) -> c e", e=CHUNK)).then_inc(loaded_idx, 16)
                sp.dma_start(dst_sb[:, :], dst_pt).then_inc(loaded_idx, 16)
                sp.dma_start(src_sb[:, :], src_pt).then_inc(loaded_idx, 16)

                def col(v):
                    return v.rearrange("(p o) -> p o", o=1)

                def row(v, n):
                    return v.rearrange("(o f) -> o f", o=1).to_broadcast([n, P])

                small = [(wg[:, l, :], w_gcn[l]) for l in range(LAYERS)]
                small += [(bg[:, l:l + 1], col(b_gcn[l])) for l in range(LAYERS)]
                small += [(w1ab[:, 0:P], msg_w[0][0:P, :]), (w1ab[:, P:2 * P], msg_w[0][P:2 * P, :]),
                          *((w1c[r * ED:(r + 1) * ED, :], msg_w[0][2 * P:2 * P + ED, :]) for r in range(3)), (w2[:, :], msg_w[1]), (w3[:, :], msg_w[2]),
                          (u1a[:, :], upd_w[0][0:P, :]), (u1b[:, :], upd_w[0][P:2 * P, :]), (u2[:, :], upd_w[1]),
                          (u3[:, :], upd_w[2]), (b1_col[:, :], col(msg_b[0])), (b2_rep[:, :], row(msg_b[1], 3)),
                          (b3_col[:, :], col(msg_b[2])), (c1_col[:, :], col(upd_b[0])), (c2_col[:, :], col(upd_b[1])),
                          (c3_row[:, :], row(upd_b[2], P)), (g_row[:, :], row(ln_g, P)), (be_row[:, :], row(ln_b, P))]
                assert len(small) == WEIGHT_LOADS
                for to, frm in small:
                    sp.dma_start(to, frm).then_inc(loaded, 16)
                sp.wait_ge(pool_done, 10)
                for part in range(3):
                    sp.dma_start(dst_table[part, NODES:COLS, :], ones_b[0:COLS - NODES, :]).then_inc(stored, 16)
                sp.wait_ge(keys_ready, 1)
                sp.dma_start(dst_short, dst_rows_s[:, :]).then_inc(stored, 16)
                sp.wait_ge(stored, 64)

            @block.scalar
            def _(act):
                act.wait_ge(loaded_idx, 48)
                act.dma_start(x_nm[:, 0:FULL, :], x[0:FULL * P, :].rearrange("(b p) f -> p b f", p=P)).then_inc(loaded_x, 16)
                act.wait_ge(pool_done, 1)
                act.dma_start(x_nm[0:REST, FULL, :], x[FULL * P:N, :]).then_inc(loaded_x, 16)
                nodes_on_act(rows_in, act)

            @block.gpsimd
            def _(pool):
                pool.memset(x_nm[:, FULL:BLOCKS, :], 0.0).then_inc(pool_done, 1)
                pool.memset(ones[:, :], 1.0).then_inc(pool_done, 1)
                pool.memset(ident[:, :], 0.0).then_inc(pool_done, 1)
                pool.wait_ge(pool_done, 3)
                pool.affine_select(out=ident[:, :], in_=ident[:, :], compare_op=ALU.not_equal, fill=1.0,
                                   base=0, pattern=[[-1, P]], channel_multiplier=1).then_inc(pool_done, 1)
                pool.iota(win_i[:, :], pattern=[[1, WIN]], base=0, channel_multiplier=0).then_inc(pool_done, 1)
                pool.iota(part_i[:, :], pattern=[[0, 1]], base=0, channel_multiplier=1).then_inc(pool_done, 1)
                pool.iota(step_i[:, :], pattern=[[WIN, MAXPASS]], base=0, channel_multiplier=0).then_inc(pool_done, 1)
                pool.iota(key_i[:, :], pattern=[[1, KEYS]], base=0, channel_multiplier=0).then_inc(pool_done, 1)
                pool.memset(eps_col[:, :], EPS).then_inc(pool_done, 1)
                pool.memset(ones_bf[:, :], 1.0)
                pool.memset(ones_b[:, :], 1.0).then_inc(pool_done, 1)
                pool.memset(shared[:, :], 0.0).then_inc(pool_done, 1)
                pool.memset(deg[:, :], 0.0)

            @block.vector
            def _(dve):
                link = Chain(dve, dve_done)
                dve.wait_ge(loaded_idx, 48)
                dve.tensor_copy(dst_f[:, :], dst_sb[:, :])
                dve.tensor_copy(dst_rows_s[:, :], dst_rows[:, :]).then_inc(keys_ready, 1)
                dve.tensor_reduce(lo_hi[:, 0:1], dst_rows[:, :], AX.X, ALU.min)
                link(dve.tensor_reduce(lo_hi[:, 1:2], dst_rows[:, :], AX.X, ALU.max))
                dve.wait_ge(pool_done, 9)
                dve.tensor_scalar(diag[:, 0, :], ident[0:CHUNKS, 0:CHUNKS], lo_hi[:, 0:1], None, ALU.mult)
                dve.tensor_scalar(diag[:, 1, :], ident[0:CHUNKS, 0:CHUNKS], lo_hi[:, 1:2], None, ALU.mult).then_inc(onehot_ready, 1)
                dve.tensor_copy(win_iota[:, :], win_i[:, :])
                dve.tensor_copy(ident_b[:, :], ident[:, :])
                dve.tensor_copy(part_iota[:, :], part_i[:, :])
                dve.tensor_copy(key_iota[:, 0:KEYS], key_i[:, :])
                dve.tensor_copy(node_iota[:, :], key_i[:, 0:P])
                link(dve.tensor_scalar(src_i[:, :], src_sb[:, :], P - 1, None, ALU.bitwise_and))
                dve.tensor_copy(src_place[:, :], src_i[:, :])
                link(dve.tensor_scalar(src_neg[:, :], src_i[:, :], -1.0, None, ALU.mult))
                link(dve.tensor_scalar(src_i[:, :], src_sb[:, :], P.bit_length() - 1, None, ALU.logical_shift_right))
                dve.tensor_copy(src_block[:, :], src_i[:, :])
                link(dve.tensor_copy(steps_f[:, :], step_i[:, :]))
                dve.wait_ge(pe_done, 1)
                link(dve.tensor_copy(lo_all[:, :], bank[7][:, 0:CHUNKS]))
                link(dve.tensor_tensor(span[:, :], bank[7][:, CHUNKS:2 * CHUNKS], lo_all[:, :], ALU.subtract))
                link(dve.tensor_reduce(span_max[:, :], span[:, :], AX.X, ALU.max))
                link(dve.tensor_scalar(over[:, :], steps_f[:, :], span_max[:, 0:1], None, ALU.is_le))
                link(dve.tensor_reduce(pass_f[:, :], over[:, :], AX.X, ALU.add))
                link(dve.tensor_copy(pass_i[:, :], pass_f[:, :]))
                link(dve.tensor_scalar(part_node[:, :], part_iota[:, :], float(WIN), -float(WIN), ALU.is_ge, ALU.mult))
                link(dve.tensor_tensor(part_node[:, :], part_node[:, :], part_iota[:, :], ALU.add))
                link(dve.tensor_scalar(span_max[:, :], part_iota[:, :], 2.0 * WIN, -float(WIN), ALU.is_ge, ALU.mult))
                link(dve.tensor_tensor(part_node[:, :], part_node[:, :], span_max[:, :], ALU.add))
                dve.wait_ge(loaded_x, 32)

                def measure_x(n, b, nb):
                    measure(rows_in, dve, n, b, nb)
                    if n == 2:
                        split_features_weights()
                    if n == 3:
                        split_bias()
                    if n >= NG - DIAG_STEPS:
                        step_of = n - (NG - DIAG_STEPS)
                        diagonal(step_of * BLOCKS // DIAG_STEPS, (step_of + 1) * BLOCKS // DIAG_STEPS)

                def split_features_weights():
                    dve.wait_ge(loaded, 16 * WEIGHT_LOADS)
                    for part in range(3):
                        link(dve.tensor_copy(w1c_parts[:, part, :], w1c[:, :]))
                        if part < 2:
                            link(dve.tensor_tensor(w1c[:, :], w1c[:, :], w1c_parts[:, part, :], ALU.subtract))

                def split_bias():
                    link(dve.tensor_copy(b2_part[:, 0, :], b2_rep[:, :]))
                    link(dve.tensor_tensor(b2_left[:, 0, :], b2_rep[:, :], b2_part[:, 0, :], ALU.subtract))
                    link(dve.tensor_copy(b2_part[:, 1, :], b2_left[:, 0, :]))
                    link(dve.tensor_tensor(b2_left[:, 1, :], b2_left[:, 0, :], b2_part[:, 1, :], ALU.subtract))
                    link(dve.tensor_copy(b2_part[:, 2, :], b2_left[:, 1, :]))
                    for s in range(3):
                        link(dve.tensor_scalar(b2_left[:, s % 2, :], b2_part[:, s, :], ident[0:3, s:s + 1], None, ALU.mult)
                             if s == 0 else
                             dve.scalar_tensor_tensor(out=b2_left[:, s % 2, :], in0=b2_part[:, s, :], scalar=ident[0:3, s:s + 1],
                                                      in1=b2_left[:, (s + 1) % 2, :], op0=ALU.mult, op1=ALU.add))
                    for t in range(TPC):
                        dve.tensor_copy(b2_split[:, t, :], b2_left[:, 0, :])

                def diagonal(first, end):
                    dve.wait_ge(pool_done, 11)
                    for b in range(first, end):
                        dve.tensor_copy(counts[:, b, cols(b, 1)], ident[:, :])

                nodes_on_dve(rows_in, dve, (0, measure_x))

            @block.tensor
            def _(pe):
                pe.wait_ge(onehot_ready, 1)
                pe.matmul(bank[7][:, 0:2 * CHUNKS], ones[0:CHUNKS, :], diag[:, :, :].rearrange("p a c -> p (a c)"),
                          start=True, stop=True).then_inc(pe_done, 1)
                nodes_on_pe(rows_in, pe)

        passes = nc.values_load(pass_i[0:1, 0:1], min_val=1, max_val=MAXPASS)

        def edge_passes(name, engines, gather=False):
            def start():
                with phase(f"{name}_start") as block:
                    @block.vector
                    def _(dve):
                        dve.memset(pass_off[:, :], 0.0)

            def windows():
                with phase(f"{name}_windows") as block:
                    @block.vector
                    def _(dve):
                        link = Chain(dve, dve_done)
                        link(dve.tensor_scalar(win_lo[:, :], lo_all[:, :], pass_off[:, 0:1], float(NODES), ALU.add, ALU.min))
                        link(dve.tensor_copy(win_lo_i[:, :], win_lo[:, :]))
                        dve.tensor_scalar(win_node[:, :], win_lo[0:3 * WIN, :], part_node[0:3 * WIN, 0:1], None, ALU.add)
                        dve.tensor_tensor(rel[:, :].rearrange("p (c t) -> p c t", t=TPC),
                                          dst_f[:, :].rearrange("p (c t) -> p c t", t=TPC),
                                          win_lo[:, :].unsqueeze(2).to_broadcast([P, CHUNKS, TPC]), ALU.subtract)
                        link(dve.tensor_scalar(pass_off[:, :], pass_off[:, :], float(WIN), None, ALU.add))
                        if name == "count":
                            count_windows(dve, link)

            start()
            with nc.Fori(0, passes):
                windows()
                with phase(f"{name}_edges", gather=gather) as block:
                    engines(block)

        def edge_engines(block, target, rows_of, messages):
            z = [bank[0], bank[1]]
            y = [bank[2], bank[3]]
            acc = [bank[4], bank[5]]

            @block.vector
            def _(dve):
                def indices(i, k):
                    if rows_of is not None:
                        dve.wait_ge(z_done if messages else seg_done, i * SLOTS + k + 1)
                        dve.tensor_copy(idx[:, k * TPC:(k + 1) * TPC],
                                        src_sb[:, bass.ds((i * SLOTS + k) * TPC, TPC)]).then_inc(idx_ready, 1)

                def prepare(i, k):
                    dve.wait_ge(seg_done, i * SLOTS + k + 1)
                    dve.tensor_tensor(
                        onehot[:, k, :, :],
                        rel[:, bass.ds((i * SLOTS + k) * TPC, TPC)].unsqueeze(2).to_broadcast([P, TPC, WIN]),
                        win_iota[:, :].unsqueeze(1).to_broadcast([P, TPC, WIN]),
                        ALU.is_equal).then_inc(onehot_ready, 1)
                    if messages:
                        dve.wait_ge(dst_bc_in[k], 16 * (i + 1))
                        dve.tensor_scalar(onehot_t[:, k, :], dst_bc[:, k, :], win_node[:, bass.ds(i * SLOTS + k, 1)],
                                          None, ALU.is_equal).then_inc(onehot_t_ready, 1)

                def add_window(i, k):
                    at = dve.value_load(win_lo_i[0:1, bass.ds(i * SLOTS + k, 1)], min_val=0, max_val=NODES)
                    dve.wait_ge(seg_done, i * SLOTS + k + 1 + SLOTS)
                    dve.wait_ge(window_added, i * SLOTS + k + 2)
                    w = target[:, bass.ds(at, WIN)]
                    dve.tensor_tensor(w, w, acc[k % 2][:, 0:WIN], ALU.add).then_inc(window_added, 1)

                def hidden_start(i):
                    dve.wait_ge(product1_done, i + 1)
                    dve.scalar_tensor_tensor(out=hidden[:, bass.ds(i * P, P)], in0=deg[:, bass.ds(i * P, P)],
                                             scalar=b3u1b_col[:, 0:1], in1=bank[6][:, 0:P],
                                             op0=ALU.mult, op1=ALU.add).then_inc(hidden1_done, 1)

                for k in range(SLOTS):
                    indices(0, k)
                    prepare(0, k)
                lag = 2 if messages else 0
                with dve.Fori(0, ITERS - 1) as i:
                    for k in range(SLOTS + lag):
                        if k >= lag:
                            add_window(i, k - lag)
                        if k < SLOTS:
                            indices(i + 1, k)
                        if k >= lag:
                            prepare(i + 1, k - lag)
                    if messages:
                        hidden_start(i)
                for k in range(SLOTS):
                    add_window(ITERS - 1, k)

            @block.gpsimd
            def _(pool):
                if rows_of is None:
                    return
                with pool.Fori(0, ITERS) as i:
                    for k in range(SLOTS):
                        pool.wait_ge(idx_ready, i * SLOTS + k + 1)
                        pool.sem_inc(gathers_begun, 1)
                        for j in range(k * TPC, (k + 1) * TPC):
                            pool.indirect_dma_start(
                                out=(rows_b if messages else rows)[:, j, :], out_offset=None, in_=rows_of,
                                in_offset=bass.IndirectOffsetOnAxis(ap=idx[:, j:j + 1].bitcast(U32), axis=0),
                            ).then_inc(gathered[j], 16)

            @block.sync
            def _(sp):
                if not messages:
                    return
                with sp.Fori(0, ITERS) as i:
                    for k in range(SLOTS):
                        c = i * SLOTS + k
                        at = sp.value_load(win_lo_i[0:1, bass.ds(c, 1)], min_val=0, max_val=NODES)
                        sp.wait_ge(z_done, c + 1)
                        sp.dma_start(dst_bc[:, k, :], dst_short[bass.ds(c, 1), :].to_broadcast([3 * WIN, CHUNK])
                                     ).then_inc(dst_bc_in[k], 16)
                        sp.dma_start(edge_in[:, k, :], edge_table[:, bass.ds(c * CHUNK, CHUNK)]).then_inc(edge_in_in[k], 16)
                        for part in range(3):
                            sp.dma_start(dst_win[part * WIN:(part + 1) * WIN, k, :],
                                         dst_table[part, bass.ds(at, WIN), :]).then_inc(dst_win_in[k], 16)

            @block.scalar
            def _(act):
                if not messages:
                    return

                def relu1(i, k):
                    act.wait_ge(z_done, i * SLOTS + k + 1 + SLOTS)
                    act.wait_ge(y_done, i * SLOTS + k + 1)
                    act.activation(r1[:, k % 2, :], z[k % 2][:, :], ACT.Relu, bias=b1_col[:, 0:1]).then_inc(relu1_done, 1)

                def relu2(i, k):
                    act.wait_ge(y_done, i * SLOTS + k + 1 + 2)
                    act.wait_ge(seg_done, i * SLOTS + k + 1)
                    act.activation(r2[:, k, :], y[k % 2][:, :], ACT.Relu).then_inc(relu2_done, 1)

                with act.Fori(0, ITERS) as i:
                    for k in range(SLOTS + 1):
                        if k < SLOTS:
                            relu1(i, k)
                        if k >= 1:
                            relu2(i, k - 1)

            @block.tensor
            def _(pe):
                pe.sem_inc(seg_done, SLOTS)
                pe.sem_inc(window_added, 2)
                if messages:
                    pe.sem_inc(hidden1_done, 1)
                    pe.sem_inc(z_done, SLOTS)
                    pe.sem_inc(relu1_done, 2)
                    pe.sem_inc(y_done, 2)
                    pe.sem_inc(relu2_done, 2)

                def first(i, k):
                    c = i * SLOTS + k
                    pe.wait_ge(relu1_done, c + 1)
                    pe.wait_ge(edge_in_in[k], 16 * (i + 1))
                    for part in range(3):
                        n = (3 - part) * ED
                        pe.matmul(z[k % 2][:, :], w1c_parts[0:n, part, :], edge_in[0:n, k, :], start=(part == 0), stop=False)
                    pe.wait_ge(dst_win_in[k], 48 * (i + 1))
                    pe.wait_ge(onehot_t_ready, c + 1)
                    pe.matmul(z[k % 2][:, :], dst_win[:, k, :], onehot_t[:, k, :], start=False, stop=False)
                    for t in range(TPC):
                        pe.wait_ge(gathered[k * TPC + t], 16 * (i + 1))
                        for part in range(3):
                            last = pe.matmul(z[k % 2][:, t * P:(t + 1) * P],
                                             rows_b[:, k * TPC + t, part * P:(part + 1) * P], ident_b[:, :],
                                             start=False, stop=(t == TPC - 1 and part == 2))
                    last.then_inc(z_done, 1)

                def second(i, k):
                    c = i * SLOTS + k
                    pe.wait_ge(relu2_done, c + 1)
                    pe.matmul(y[k % 2][:, :], ones_bf[:, :], b2_split[:, :, :].rearrange("p t f -> p (t f)"),
                              start=True, stop=False)
                    pe.wait_ge(relu1_done, c + 1 + 2)
                    for t in range(TPC):
                        last = pe.matmul(y[k % 2][:, t * P:(t + 1) * P], r1[:, k % 2, t * P:(t + 1) * P], w2[:, :],
                                         start=False, stop=(t == TPC - 1))
                    last.then_inc(y_done, 1)

                def summed(i, k):
                    c = i * SLOTS + k
                    pe.wait_ge(onehot_ready, c + 1)
                    pe.wait_ge(window_added, c + 1)
                    if messages:
                        pe.wait_ge(relu2_done, c + 1 + 2)
                    for t in range(TPC):
                        if messages:
                            what = r2[:, k, t * P:(t + 1) * P]
                        elif rows_of is not None:
                            pe.wait_ge(gathered[k * TPC + t], 16 * (i + 1))
                            what = rows[:, k * TPC + t, :]
                        else:
                            what = ones[:, :]
                        last = pe.matmul(acc[k % 2][:, 0:WIN], what, onehot[:, k, t, :],
                                         start=(t == 0), stop=(t == TPC - 1))
                    last.then_inc(seg_done, 1)

                def iteration(i, block_left):
                    for k in range(SLOTS + 2):
                        if messages and k < SLOTS:
                            first(i, k)
                        if messages and 1 <= k <= SLOTS:
                            second(i, k - 1)
                        if k >= 2:
                            summed(i, k - 2)
                        if messages and block_left and k == 2:
                            pe.wait_ge(hidden1_done, i + 1)
                            pe.matmul(bank[6][:, 0:P], u1a[:, :], h_fm[:, bass.ds(i * P, P)],
                                      start=True, stop=True).then_inc(product1_done, 1)

                with pe.Fori(0, ITERS - 1) as i:
                    iteration(i, True)
                iteration(ITERS - 1, False)

        def count_windows(dve, link):
            dve.tensor_scalar(win_word[:, :], win_lo_i[:, :], 2, None, ALU.logical_shift_right)
            link(dve.tensor_scalar(low_bits[:, :], win_lo_i[:, :], 3, None, ALU.bitwise_and))
            dve.tensor_copy(win_shift[:, :], low_bits[:, :])
            dve.tensor_scalar(inside[:, 0, :], rel[:, :], 0.0, None, ALU.is_ge)
            link(dve.scalar_tensor_tensor(out=key[:, :], in0=src_block[:, :], scalar=float(CWIN), in1=rel[:, :],
                                          op0=ALU.mult, op1=ALU.add))
            key_ct = key[:, :].rearrange("p (c t) -> p c t", t=TPC)
            link(dve.tensor_tensor(key_ct, key_ct, win_shift[:, :].unsqueeze(2).to_broadcast([P, CHUNKS, TPC]), ALU.add))
            link(dve.tensor_scalar(inside[:, 1, :], rel[:, :], float(WIN), None, ALU.is_lt))
            link(dve.tensor_tensor(inside[:, 0, :], inside[:, 0, :], inside[:, 1, :], ALU.mult))
            link(dve.scalar_tensor_tensor(out=key[:, :], in0=key[:, :], scalar=1.0, in1=inside[:, 0, :],
                                          op0=ALU.add, op1=ALU.mult))
            dve.tensor_scalar(key[:, :], key[:, :], -1.0, None, ALU.add)

        def count_engines(block):
            sums = [[bank[0], bank[1], bank[2]], [bank[3], bank[4], bank[5]]]
            degs = [bank[6], bank[7]]

            @block.vector
            def _(dve):
                def prepare(i, k):
                    c = i * SLOTS + k
                    dve.wait_ge(counted, c + 1)
                    for t in range(TPC):
                        at = bass.ds(c * TPC + t, 1)
                        dve.tensor_scalar(key_onehot[:, k % 2, t, 0:KEYS], key_iota[:, 0:KEYS], key[:, at], None, ALU.is_equal)
                        if t < SRC_ON_DVE:
                            dve.tensor_scalar(src_onehot[:, k % 2, t, :], key_iota[:, 0:P], src_place[:, at], None, ALU.is_equal)
                    dve.tensor_tensor(
                        win_onehot[:, k % 2, :, :],
                        rel[:, bass.ds(c * TPC, TPC)].unsqueeze(2).to_broadcast([P, TPC, WIN]),
                        win_iota[:, :].unsqueeze(1).to_broadcast([P, TPC, WIN]),
                        ALU.is_equal).then_inc(keys_ready, 1)

                def add_degrees(i, k):
                    c = i * SLOTS + k
                    at = dve.value_load(win_lo_i[0:1, bass.ds(c, 1)], min_val=0, max_val=NODES)
                    dve.wait_ge(degrees_counted, c + 1)
                    dve.wait_ge(degrees_added, c + 2)
                    w = deg[:, bass.ds(at, WIN)]
                    dve.tensor_tensor(w, w, degs[k % 2][:, 0:WIN], ALU.add).then_inc(degrees_added, 1)

                prepare(0, 0)
                with dve.Fori(0, ITERS - 1) as i:
                    for k in range(SLOTS):
                        prepare(i + (k + 1) // SLOTS, (k + 1) % SLOTS)
                        add_degrees(i, k)
                for k in range(SLOTS):
                    if k + 1 < SLOTS:
                        prepare(ITERS - 1, k + 1)
                    add_degrees(ITERS - 1, k)

            @block.tensor
            def _(pe):
                pe.sem_inc(counted, 2)
                pe.sem_inc(degrees_added, 2)
                pe.sem_inc(sums_copied, 2)
                pe.sem_inc(window_added, 2)
                with pe.Fori(0, ITERS) as i:
                    for k in range(SLOTS):
                        c = i * SLOTS + k
                        pe.wait_ge(keys_ready, c + 1)
                        pe.wait_ge(degrees_added, c + 1)
                        pe.wait_ge(sums_copied, c + 1)
                        for t in range(TPC):
                            last = pe.matmul(degs[k % 2][:, 0:WIN], ones_b[:, :], win_onehot[:, k % 2, t, :],
                                      start=(t == 0), stop=(t == TPC - 1))
                        last.then_inc(degrees_counted, 1)
                        pe.wait_ge(onehot_ready, c + 1)
                        for h, (b, nb) in enumerate(THIRDS):
                            for t in range(TPC):
                                last = pe.matmul(sums[k % 2][h][:, 0:nb * CWIN], src_onehot[:, k % 2, t, :],
                                                 key_onehot[:, k % 2, t, b * CWIN:(b + nb) * CWIN],
                                                 start=(t == 0), stop=(t == TPC - 1))
                        last.then_inc(counted, 1)

            @block.scalar
            def _(act):
                def sources(c, k):
                    act.wait_ge(counted, c + 1)
                    for t in range(SRC_ON_DVE, TPC):
                        ins = act.activation(squares[:, k % 2, t, :], node_iota[:, :], ACT.Square,
                                             bias=src_neg[:, bass.ds(c * TPC + t, 1)])
                    ins.then_inc(squared, 1)
                    act.wait_ge(squared, c + 1)
                    act.activation(src_onehot[:, k % 2, SRC_ON_DVE:, :], squares[:, k % 2, SRC_ON_DVE:, :], ACT.Relu,
                                   bias=1.0, scale=-1.0).then_inc(onehot_ready, 1)

                def copy_sums(c, k):
                    act.wait_ge(counted, c + 1 + 2)
                    act.wait_ge(window_added, c + 1)
                    for h, (b, nb) in enumerate(THIRDS):
                        ins = act.activation(sum_bytes[:, k % 2, b * CWIN:(b + nb) * CWIN], sums[k % 2][h][:, 0:nb * CWIN],
                                             ACT.Copy)
                    ins.then_inc(sums_copied, 1)

                sources(0, 0)
                with act.Fori(0, ITERS - 1) as i:
                    for k in range(SLOTS):
                        sources(i * SLOTS + k + 1, (k + 1) % SLOTS)
                        copy_sums(i * SLOTS + k, k)
                for k in range(SLOTS):
                    if k + 1 < SLOTS:
                        sources((ITERS - 1) * SLOTS + k + 1, k + 1)
                    copy_sums((ITERS - 1) * SLOTS + k, k)

            @block.gpsimd
            def _(pool):
                with pool.Fori(0, ITERS) as i:
                    for k in range(SLOTS):
                        c = i * SLOTS + k
                        at = pool.value_load(win_word[0:1, bass.ds(c, 1)], min_val=0, max_val=NODES // 4)
                        pool.wait_ge(sums_copied, c + 1 + 2)
                        pool.wait_ge(window_added, c + 2)
                        w = count_words[:, :, bass.ds(at, CWIN // 4)]
                        pool.tensor_tensor(w, w, sum_words[:, k % 2, :, :], ALU.add).then_inc(window_added, 1)

        edge_passes("count", count_engines)

        SPLIT_DMAS = QUARTERS * 16

        def split_on_pool(pool):
            with pool.Fori(0, LAYER_STEP + 1) as i:
                pool.wait_ge(feat_in, 16 * (i + 1))
                pool.sem_inc(split_begun, 1)
                pool.tensor_copy(feat_parts[:, 0, :], feat).then_inc(feat_split, 1)
                pool.wait_ge(feat_split, i * 4 + 1)
                pool.tensor_tensor(feat, feat, feat_parts[:, 0, :], ALU.subtract).then_inc(feat_split, 1)
                pool.wait_ge(feat_split, i * 4 + 2)
                pool.sem_inc(split_begun, 1)
                pool.tensor_copy(feat_parts[:, 1, :], feat).then_inc(feat_split, 1)
                pool.wait_ge(feat_split, i * 4 + 3)
                pool.tensor_tensor(feat_parts[:, 2, :], feat, feat_parts[:, 1, :], ALU.subtract).then_inc(feat_split, 1)

        def split_on_sync(sp, layer):
            sp.sem_inc(feat_stored, 3 * SPLIT_DMAS)
            with sp.Fori(0, LAYER_STEP + 1) as i:
                r = layer * LAYER_STEP + i
                sp.wait_ge(feat_stored, 3 * SPLIT_DMAS * (i + 1))
                sp.sem_inc(split_begun, 1)
                sp.dma_start(feat, edge_q[:, bass.ds(r * SPLIT, SPLIT)]).then_inc(feat_in, 16)
                for part, ready in enumerate((1, 3, 4)):
                    sp.wait_ge(feat_split, i * 4 + ready)
                    sp.sem_inc(split_begun, 1)
                    for q in range(QUARTERS):
                        sp.dma_start(edge_table[part * ED:(part + 1) * ED, bass.ds(r * SPLIT + q * QCOLS, SPLIT)],
                                     feat_parts[q * ED:(q + 1) * ED, part, :]).then_inc(feat_stored, 16)
            sp.wait_ge(feat_stored, 3 * SPLIT_DMAS * (LAYER_STEP + 2))

        def convert(eng, b, act):
            eng.wait_ge(block_used, b + 1)
            to, frm = counts_bf[:, b % 2, :], counts[:, b, 0:NODES]
            ins = eng.activation(to, frm, ACT.Copy) if act else eng.tensor_copy(to, frm)
            ins.then_inc(block_ready[b % 2], 1)

        with phase("degree") as block:
            @block.tensor
            def _(pe):
                for n, (b, nb) in enumerate(GROUPS):
                    for t in range(nb):
                        last = pe.transpose(bank[n][:, t * P:(t + 1) * P], deg[:, cols(b + t, 1)], ident[:, :])
                    last.then_inc(pe_done, 1)
                pe.transpose(bank[7][:, 0:P], w3[:, :], ident[:, :])
                pe.matmul(bank[7][:, P:P + 1], u1b[:, :], b3_col[:, :], start=True, stop=True).then_inc(turned, 1)
                pe.wait_ge(columns_ready, 1)
                pe.matmul(bank[7][:, 2 * P:3 * P], w3_turned[:, :], u1b[:, :], start=True, stop=True).then_inc(products_ready, 1)
                for n, (b, nb) in enumerate(GROUPS):
                    pe.wait_ge(keys_ready, n + 1)
                    for t in range(nb):
                        last = pe.matmul(bank[n][:, t * P:(t + 1) * P], ones[:, :], dinv_diag[:, b + t, :],
                                         start=True, stop=True)
                    last.then_inc(pe2_done, 1)

            @block.scalar
            def _(act):
                for n, (b, nb) in enumerate(GROUPS):
                    act.wait_ge(pe_done, n + 1)
                    act.activation(dinv_nm[:, b:b + nb], group(bank[n][:, 0:nb * P])[:, :, 0], ACT.Sqrt, bias=1.0).then_inc(act_done, 1)
                act.wait_ge(turned, 1)
                act.activation(b3u1b_col[:, :], bank[7][:, P:P + 1], ACT.Copy)
                act.activation(w3_turned[:, :], bank[7][:, 0:P], ACT.Copy).then_inc(columns_ready, 1)
                act.wait_ge(products_ready, 1)
                act.activation(w3u1b[:, :], bank[7][:, 2 * P:3 * P], ACT.Copy)
                for n, (b, nb) in enumerate(GROUPS):
                    act.wait_ge(pe2_done, n + 1)
                    act.activation(dinv[:, cols(b, nb)], bank[n][:, 0:nb * P], ACT.Copy).then_inc(relu1_done, 1)

            @block.vector
            def _(dve):
                link = Chain(dve, dve_done)

                def scale(n, b, nb):
                    dve.wait_ge(relu1_done, n + 1)
                    dve.tensor_tensor(h_fm[:, cols(b, nb)], h_fm[:, cols(b, nb)], dinv[:, cols(b, nb)], ALU.mult)

                for n, (b, nb) in enumerate(GROUPS):
                    dve.wait_ge(act_done, n + 1)
                    link(dve.reciprocal(dinv_nm[:, b:b + nb], dinv_nm[:, b:b + nb]))
                    for t in range(b, b + nb):
                        ins = dve.tensor_scalar(dinv_diag[:, t, :], ident[:, :], dinv_nm[:, t:t + 1], None, ALU.mult)
                    ins.then_inc(keys_ready, 1)
                link(dve.tensor_reduce(deg_max[:, :], deg[:, 0:N], AX.X, ALU.max))
                dve.tensor_scalar(sparse_i[:, :], deg_max[:, :], float(DENSE_MAX), None, ALU.is_gt)
                for n, (b, nb) in enumerate(GROUPS):
                    scale(n, b, nb)

        sparse = nc.values_load(sparse_i[0:1, 0:1], min_val=0, max_val=1)

        with nc.Fori(0, LAYERS) as layer:
            with nc.If(sparse < 1):
                with phase("gcn_dense") as block:
                    @block.tensor
                    def _(pe):
                        def rows_out(n):
                            b, nb = GROUPS[n]
                            if n >= 1:
                                pe.wait_ge(y_done, n)
                            for t in range(nb):
                                last = pe.matmul(bank[7][:, t * P:(t + 1) * P], h_fm[:, cols(b + t, 1)],
                                                 wg[:, bass.ds(layer, 1), :].rearrange("p o f -> p (o f)"),
                                                 start=True, stop=True)
                            last.then_inc(pe_done, 1)

                        def sums_of(n):
                            b, nb = GROUPS[n]
                            pe.wait_ge(relu2_done, n + 1)
                            for s in range(b, min(b + nb, BLOCKS - 1)):
                                pe.wait_ge(block_ready[s % 2], s // 2 + 1)
                                for part in range(2 if s == BLOCKS - 2 else 3):
                                    for m, (g, ng) in enumerate(GROUPS):
                                        last = pe.matmul(bank[m][:, 0:ng * P], parts[:, s, part, :],
                                                         counts_bf[:, s % 2, cols(g, ng)],
                                                         start=(s == 0 and part == 0), stop=False)
                                last.then_inc(block_used, 1)

                        def last_sums():
                            pe.wait_ge(block_ready[(BLOCKS - 1) % 2], (BLOCKS - 1) // 2 + 1)
                            for m, (g, ng) in enumerate(GROUPS):
                                for s, part in ((BLOCKS - 2, 2), (BLOCKS - 1, 0), (BLOCKS - 1, 1), (BLOCKS - 1, 2)):
                                    last = pe.matmul(bank[m][:, 0:ng * P], parts[:, s, part, :],
                                                     counts_bf[:, s % 2, cols(g, ng)],
                                                     start=False, stop=(s == BLOCKS - 1 and part == 2))
                                last.then_inc(counted, 1)

                        pe.sem_inc(block_used, 2)
                        rows_out(0)
                        for n in range(NG):
                            if n + 1 < NG:
                                rows_out(n + 1)
                            sums_of(n)
                        last_sums()

                    @block.gpsimd
                    def _(pool):
                        split_on_pool(pool)

                    @block.sync
                    def _(sp):
                        split_on_sync(sp, layer)

                    @block.scalar
                    def _(act):
                        act.activation(bg_now[:, :], bg[:, bass.ds(layer, 1)], ACT.Copy).then_inc(act_done, 1)
                        for n, (b, nb) in enumerate(GROUPS):
                            act.wait_ge(pe_done, n + 1)
                            act.activation(parts[:, b:b + nb, 0, :], group(bank[7][:, 0:nb * P]), ACT.Copy).then_inc(relu1_done, 1)
                            act.wait_ge(y_done, n + 1)
                            act.activation(parts[:, b:b + nb, 1, :], group(part_left[:, n % 2, 0:nb * P]), ACT.Copy).then_inc(relu1_done, 1)
                            for s in range(b, b + nb):
                                if s % 2 == 0:
                                    convert(act, s, True)
                        act.wait_ge(act_done, 1)
                        for n, (b, nb) in enumerate(GROUPS):
                            act.wait_ge(dve_done, n + 1)
                            act.activation(h_fm[:, cols(b, nb)], agg[:, cols(b, nb)], ACT.Relu,
                                           bias=bg_now[:, 0:1]).then_inc(relued, 1)

                    @block.vector
                    def _(dve):
                        for n, (b, nb) in enumerate(GROUPS):
                            dve.wait_ge(relu1_done, 2 * n + 1)
                            dve.tensor_tensor(group(part_left[:, n % 2, 0:nb * P]), group(bank[7][:, 0:nb * P]), parts[:, b:b + nb, 0, :],
                                              ALU.subtract).then_inc(y_done, 1)
                            dve.wait_ge(relu1_done, 2 * n + 2)
                            dve.tensor_tensor(parts[:, b:b + nb, 2, :], group(part_left[:, n % 2, 0:nb * P]), parts[:, b:b + nb, 1, :],
                                              ALU.subtract).then_inc(relu2_done, 1)
                            for s in range(b, b + nb):
                                if s % 2 == 1:
                                    convert(dve, s, False)
                        def scale(n):
                            b, nb = GROUPS[n]
                            dve.wait_ge(relued, n + 1)
                            dve.tensor_tensor(h_fm[:, cols(b, nb)], h_fm[:, cols(b, nb)], dinv[:, cols(b, nb)], ALU.mult)

                        for n, (b, nb) in enumerate(GROUPS):
                            dve.wait_ge(counted, n + 1)
                            dve.tensor_tensor(agg[:, cols(b, nb)], bank[n][:, 0:nb * P], dinv[:, cols(b, nb)],
                                              ALU.mult).then_inc(dve_done, 1)
                            if n >= 1:
                                scale(n - 1)
                        scale(NG - 1)

            with nc.Else():
                with phase("gcn_table") as block:
                    @block.gpsimd
                    def _(pool):
                        pool.memset(agg[:, NODES:COLS], 0.0)
                        split_on_pool(pool)

                    @block.scalar
                    def _(act):
                        act.activation(wg_now[:, :], wg[:, bass.ds(layer, 1), :].rearrange("p o f -> p (o f)"), ACT.Copy).then_inc(act_done, 1)
                        act.activation(bg_now[:, :], bg[:, bass.ds(layer, 1)], ACT.Copy)
                        for n, (b, nb) in enumerate(GROUPS):
                            act.wait_ge(pe_done, n + 1)
                            act.activation(stage[:, b:b + nb, :].rearrange("p b f -> p (b f)"), bank[n % 4][:, 0:nb * P],
                                           ACT.Copy).then_inc(relu1_done, 1)

                    @block.tensor
                    def _(pe):
                        pe.wait_ge(act_done, 1)
                        for n, (b, nb) in enumerate(GROUPS):
                            if n >= 4:
                                pe.wait_ge(relu1_done, n - 3)
                            for t in range(nb):
                                last = pe.matmul(bank[n % 4][:, t * P:(t + 1) * P], h_fm[:, cols(b + t, 1)], wg_now[:, :],
                                                 start=True, stop=True)
                            last.then_inc(pe_done, 1)
                            if n >= 4:
                                pe.wait_ge(dve_done, n - 3)
                            pe.matmul(bank[4 + n % 4][:, 0:nb * P], wg_now[:, :], h_fm[:, cols(b, nb)],
                                      start=True, stop=True).then_inc(pe2_done, 1)

                    @block.vector
                    def _(dve):
                        for n, (b, nb) in enumerate(GROUPS):
                            dve.wait_ge(pe2_done, n + 1)
                            dve.tensor_copy(agg[:, cols(b, nb)], bank[4 + n % 4][:, 0:nb * P]).then_inc(dve_done, 1)

                    @block.sync
                    def _(sp):
                        for n, (b, nb) in enumerate(GROUPS):
                            sp.wait_ge(relu1_done, n + 1)
                            sp.dma_start(table[cols(b, nb), :].rearrange("(b p) f -> p b f", p=P),
                                         stage[:, b:b + nb, :]).then_inc(stored, 16)
                        sp.wait_ge(stored, 16 * NG)
                        split_on_sync(sp, layer)

                edge_passes("gcn", lambda block: edge_engines(block, agg, table, False), gather=True)

                with phase("gcn_act") as block:
                    @block.vector
                    def _(dve):
                        for n, (b, nb) in enumerate(GROUPS):
                            dve.tensor_tensor(agg[:, cols(b, nb)], agg[:, cols(b, nb)], dinv[:, cols(b, nb)],
                                              ALU.mult).then_inc(dve_done, 1)
                        for n, (b, nb) in enumerate(GROUPS):
                            dve.wait_ge(act_done, n + 1)
                            dve.tensor_tensor(h_fm[:, cols(b, nb)], h_fm[:, cols(b, nb)], dinv[:, cols(b, nb)], ALU.mult)

                    @block.scalar
                    def _(act):
                        for n, (b, nb) in enumerate(GROUPS):
                            act.wait_ge(dve_done, n + 1)
                            act.activation(h_fm[:, cols(b, nb)], agg[:, cols(b, nb)], ACT.Relu,
                                           bias=bg_now[:, 0:1]).then_inc(act_done, 1)

        nodes = node_stages(1, x_nm, tables=True)
        with phase("gcn_out") as block:
            @block.sync
            def _(sp):
                sp.dma_start(x_nm[:, 0:XB, :], x[0:XB * P, :].rearrange("(b p) f -> p b f", p=P)).then_inc(loaded_x, 16)
                nodes_on_sync(nodes, sp)

            @block.scalar
            def _(act):
                def biased_of(n, b, nb):
                    act.activation(agg[:, cols(b, nb)], agg[:, cols(b, nb)], ACT.Identity,
                                   bias=bg_now[:, 0:1]).then_inc(biased, 1)

                nodes_on_act(nodes, act, (0, biased_of))

            @block.tensor
            def _(pe):
                def turn_sums(n, b, nb):
                    pe.wait_ge(biased, n + 1)
                    if n >= 1:
                        pe.wait_ge(updated, n)
                    for t in range(nb):
                        last = pe.transpose(bank[0][:, t * P:(t + 1) * P], agg[:, cols(b + t, 1)], ident[:, :])
                    last.then_inc(sums_read, 1)

                nodes_on_pe(nodes, pe, (1, turn_sums))

            @block.vector
            def _(dve):
                def add_sums(n, b, nb):
                    dve.wait_ge(sums_read, n + 1)
                    x_of = x_nm[:, b:b + nb, :].rearrange("p b f -> p (b f)")
                    dve.tensor_tensor(x_of, x_of, bank[0][:, 0:nb * P], ALU.add).then_inc(updated, 1)
                    dve.wait_ge(updated, n + 1)
                    measure(nodes, dve, n, b, nb)

                dve.wait_ge(loaded_x, 16)
                nodes_on_dve(nodes, dve, (1, add_sums))

            @block.gpsimd
            def _(pool):
                nodes_on_pool(nodes, pool)

        def step(last):
            end = "_last" if last else ""
            edge_passes("mp" + end, lambda block: edge_engines(block, agg, src_table, True), gather=True)

            with phase("update" + end) as block:
                nodes = node_stages(2, h_nm, gain=True, tables=not last, final=last)

                @block.tensor
                def _(pe):
                    def hidden1(n, b, nb):
                        if n >= 1:
                            pe.wait_ge(hidden1_summed, n)
                        pe.matmul(bank[0][:, 0:nb * P], w3u1b[:, :], agg[:, cols(b, nb)], start=True, stop=True).then_inc(sums_read, 1)

                    def hidden2(n, b, nb):
                        if n >= 1:
                            pe.wait_ge(hidden2_done, n)
                        pe.wait_ge(hidden1_done, n + 1)
                        pe.matmul(bank[2][:, 0:nb * P], u2[:, :], t2[:, n % 2, 0:nb * P], start=True, stop=True).then_inc(product2_done, 1)

                    def update(n, b, nb):
                        if n >= 1:
                            pe.wait_ge(updated, n)
                        pe.wait_ge(hidden2_done, n + 1)
                        for t in range(nb):
                            ins = pe.matmul(bank[3][:, t * P:(t + 1) * P], t2[:, 2 + n % 2, t * P:(t + 1) * P], u3[:, :],
                                            start=True, stop=True)
                        ins.then_inc(product3_done, 1)

                    nodes_on_pe(nodes, pe, (0, hidden1), (1, hidden2), (2, update))

                @block.gpsimd
                def _(pool):
                    def add_c3(n, b, nb):
                        pool.tensor_tensor(h_nm[:, b:b + nb, :], h_nm[:, b:b + nb, :],
                                           c3_row[:, :].unsqueeze(1).to_broadcast([P, nb, P]), ALU.add).then_inc(biased, 1)

                    nodes_on_pool(nodes, pool, (0, add_c3))

                @block.vector
                def _(dve):
                    def hidden1(n, b, nb):
                        dve.wait_ge(sums_read, n + 1)
                        to = hidden[:, cols(b, nb)]
                        dve.tensor_tensor(to, to, bank[0][:, 0:nb * P], ALU.add).then_inc(hidden1_summed, 1)

                    def update(n, b, nb):
                        dve.wait_ge(biased, n + 1)
                        dve.wait_ge(product3_done, n + 1)
                        h = h_nm[:, b:b + nb, :].rearrange("p b f -> p (b f)")
                        dve.tensor_tensor(h, h, bank[3][:, 0:nb * P], ALU.add).then_inc(updated, 1)
                        dve.wait_ge(updated, n + 1)
                        measure(nodes, dve, n, b, nb)

                    nodes_on_dve(nodes, dve, (0, hidden1), (2, update))

                @block.scalar
                def _(act):
                    def hidden1(n, b, nb):
                        act.wait_ge(hidden1_summed, n + 1)
                        if n >= 2:
                            act.wait_ge(product2_done, n - 1)
                        act.activation(t2[:, n % 2, 0:nb * P], hidden[:, cols(b, nb)], ACT.Relu,
                                       bias=c1_col[:, 0:1]).then_inc(hidden1_done, 1)

                    def hidden2(n, b, nb):
                        act.wait_ge(product2_done, n + 1)
                        if n >= 2:
                            act.wait_ge(product3_done, n - 1)
                        act.activation(t2[:, 2 + n % 2, 0:nb * P], bank[2][:, 0:nb * P], ACT.Relu,
                                       bias=c2_col[:, 0:1]).then_inc(hidden2_done, 1)

                    nodes_on_act(nodes, act, (0, hidden1), (1, hidden2))

                @block.sync
                def _(sp):
                    nodes_on_sync(nodes, sp)

        with nc.Fori(0, STEPS - 1) as _step:
            step(last=False)
        step(last=True)


def kernel(**inputs):
    import numpy as np
    import concourse.bacc as bacc
    from concourse.bass_utils import run_bass_kernel_spmd

    a = {k: np.asarray(v) for k, v in inputs.items()}
    n, d = a["x"].shape
    edges = a["src"].shape[0]
    group = SLOTS * CHUNK
    padded = -(-edges // group) * group
    src = np.zeros(padded, a["src"].dtype)
    src[:edges] = a["src"]
    dst = np.full(padded, n, a["dst"].dtype)
    dst[:edges] = a["dst"]
    features = a["edge_attr_32"].shape[1]
    edge_t = np.zeros((features, padded), a["edge_attr_32"].dtype)
    edge_t[:, :edges] = a["edge_attr_32"].T
    quarters = P // features
    edge_q = edge_t.reshape(features, quarters, -1).transpose(1, 0, 2).reshape(P, -1)
    arrays = {
        "x": a["x"],
        "src_pt": np.ascontiguousarray(src.reshape(-1, P).T),
        "dst_pt": np.ascontiguousarray(dst.reshape(-1, P).T),
        "dst_flat": dst,
        "edge_q": np.ascontiguousarray(edge_q),
    }
    groups = {
        "w_gcn": [f"L0_gnn_W{i}" for i in (1, 2, 3)], "b_gcn": [f"L0_gnn_b{i}" for i in (1, 2, 3)],
        "msg_w": [f"L1_gnn_msg_w{i}" for i in (1, 2, 3)], "msg_b": [f"L1_gnn_msg_b{i}" for i in (1, 2, 3)],
        "upd_w": [f"L1_gnn_upd_w{i}" for i in (1, 2, 3)], "upd_b": [f"L1_gnn_upd_b{i}" for i in (1, 2, 3)],
    }
    for names in groups.values():
        arrays |= {name: a[name] for name in names}
    arrays |= {"ln_g": a["L1_gnn_ln_g"], "ln_b": a["L1_gnn_ln_b"]}

    nc = bacc.Bacc("TRN2", target_bir_lowering=False, num_devices=1)
    aps = {k: nc.dram_tensor(f"in_{k}", v.shape, mybir.dt.from_np(v.dtype), kind="ExternalInput").ap()
           for k, v in arrays.items()}
    out = nc.dram_tensor("out", (n, d), F32, kind="ExternalOutput").ap()
    gnn_program(nc, aps["x"], aps["src_pt"], aps["dst_pt"], aps["dst_flat"], aps["edge_q"],
                *([aps[name] for name in names] for names in groups.values()), aps["ln_g"], aps["ln_b"], out)
    r = run_bass_kernel_spmd(nc, [{f"in_{k}": v for k, v in arrays.items()}], core_ids=[0])
    return r.results[0]["out"]
```
